# Optimizing a Trainium2 kernel written in Bass

```python
import numpy as np
import jax
import jax.numpy as jnp

def _softmax(x, axis=-1):
    return jax.nn.softmax(x, axis=axis)

def _gelu(x):
    return jax.nn.gelu(x, approximate=True)

def _silu(x):
    return jax.nn.silu(x)

def _sigmoid(x):
    return jax.nn.sigmoid(x)

def _layernorm(x, axis=-1, eps=1e-05):
    m = jnp.mean(x, axis=axis, keepdims=True)
    v = jnp.var(x, axis=axis, keepdims=True)
    return (x - m) / jnp.sqrt(v + eps)

def _scatter_add(tgt, idx, src, axis=0):
    return tgt.at[idx].add(src)

def _segment_sum(src, seg, n):
    return jax.ops.segment_sum(src, seg, n)
kernel_name = 'mk_gnn_preln_d2_gnn_r8_3f4450'

def setup_inputs(seed: int=0):
    np.random.seed(seed)
    _w = jnp.asarray

    def _rec_inputs():
        import jax
        import jax.numpy as jnp
        _gk = jax.random.key(seed)
        x = -0.000202 + 1 * jax.random.normal(jax.random.fold_in(_gk, 1), (6250, 128), jnp.float32)
        _s = jax.random.randint(jax.random.fold_in(_gk, 2), (100000,), 0, 6250, jnp.int32)
        _d = jax.random.randint(jax.random.fold_in(_gk, 3), (100000,), 0, 6250, jnp.int32)
        _loop = jnp.arange(6250, dtype=jnp.int32)
        src = jnp.concatenate([_s, _d, _loop])
        dst = jnp.concatenate([_d, _s, _loop])
        _o = jnp.argsort(dst, stable=True)
        src = src[_o]
        dst = dst[_o]
        edge_type_16 = jax.random.randint(jax.random.fold_in(_gk, 12), (206250,), 0, 16, jnp.int32)
        return (x, src, dst, edge_type_16)
    x, src, dst, edge_type_16 = _rec_inputs()

    def _L0_gnn_setup():
        import jax, jax.numpy as jnp
        import numpy as np
        N_NODES = 6250
        N_EDGES = 200000
        D_IN = 128
        D_OUT = 128
        key = jax.random.key(seed)
        k1, k2, k3, k4 = jax.random.split(key, 4)
        x = jax.random.normal(k1, (N_NODES, D_IN), dtype=jnp.float32)
        edge_index = jax.random.randint(k2, (2, N_EDGES), 0, N_NODES, dtype=jnp.int64)
        bound = 1.0 / np.sqrt(D_IN)
        W = jax.random.uniform(k3, (D_OUT, D_IN), dtype=jnp.float32, minval=-bound, maxval=bound)
        b = jax.random.uniform(k4, (D_OUT,), dtype=jnp.float32, minval=-bound, maxval=bound)
        return {'x': x, 'edge_index': edge_index, 'W': W, 'b': b}
    _L0_gnn_all = _L0_gnn_setup()
    _L0_gnn_in = {k: v for k, v in _L0_gnn_all.items() if k in ('W', 'b')}
    del _L0_gnn_all

    def _L1_gnn_setup():
        import jax, jax.numpy as jnp
        import numpy as np
        N, H = (6250, 128)
        E = 100000
        ETD = 32
        NUM_ET = 16
        LN_EPS = 1e-05
        key = jax.random.key(seed)
        ks = jax.random.split(key, 9)
        x = jax.random.normal(ks[0], (N, H), dtype=jnp.float32)
        edge_index = jax.random.randint(ks[1], (2, E), 0, N, dtype=jnp.int64)
        edge_type = jax.random.randint(ks[2], (E,), 0, NUM_ET, dtype=jnp.int64)
        edge_emb_W = jax.random.normal(ks[3], (NUM_ET, ETD), dtype=jnp.float32)
        lim_msg = 1.0 / np.sqrt(H + ETD)
        msg_W = jax.random.uniform(ks[4], (H, H + ETD), jnp.float32, -lim_msg, lim_msg)
        msg_b = jax.random.uniform(ks[5], (H,), jnp.float32, -lim_msg, lim_msg)
        lim_upd = 1.0 / np.sqrt(H)
        upd_W = jax.random.uniform(ks[6], (H, H), jnp.float32, -lim_upd, lim_upd)
        upd_b = jax.random.uniform(ks[7], (H,), jnp.float32, -lim_upd, lim_upd)
        ln_g = jnp.ones((H,), jnp.float32)
        ln_b = jnp.zeros((H,), jnp.float32)
        return {'x': x, 'edge_index': edge_index, 'edge_type': edge_type, 'edge_emb_W': edge_emb_W, 'msg_W': msg_W, 'msg_b': msg_b, 'upd_W': upd_W, 'upd_b': upd_b, 'ln_g': ln_g, 'ln_b': ln_b}
    _L1_gnn_all = _L1_gnn_setup()
    _L1_gnn_in = {k: v for k, v in _L1_gnn_all.items() if k in ('edge_emb_W', 'msg_W', 'msg_b', 'upd_W', 'upd_b', 'ln_g', 'ln_b')}
    del _L1_gnn_all
    return {'x': x, 'src': src, 'dst': dst, 'edge_type_16': edge_type_16, 'L0_gnn_W': _L0_gnn_in['W'], 'L0_gnn_b': _L0_gnn_in['b'], 'L1_gnn_edge_emb_W': _L1_gnn_in['edge_emb_W'], 'L1_gnn_msg_W': _L1_gnn_in['msg_W'], 'L1_gnn_msg_b': _L1_gnn_in['msg_b'], 'L1_gnn_upd_W': _L1_gnn_in['upd_W'], 'L1_gnn_upd_b': _L1_gnn_in['upd_b'], 'L1_gnn_ln_g': _L1_gnn_in['ln_g'], 'L1_gnn_ln_b': _L1_gnn_in['ln_b']}

def reference(x, src, dst, edge_type_16, L0_gnn_W, L0_gnn_b, L1_gnn_edge_emb_W, L1_gnn_msg_W, L1_gnn_msg_b, L1_gnn_upd_W, L1_gnn_upd_b, L1_gnn_ln_g, L1_gnn_ln_b):
    import jax
    import jax.numpy as jnp

    def _L0_gnn_ref(x, edge_index, W, b):
        import jax, jax.numpy as jnp
        import numpy as np
        N_NODES = 6250
        N_EDGES = 200000
        D_IN = 128
        D_OUT = 128
        row, col = (edge_index[0], edge_index[1])
        h = x @ W.T + b
        sums = jax.ops.segment_sum(h[row], col, num_segments=N_NODES)
        counts = jax.ops.segment_sum(jnp.ones_like(col, dtype=h.dtype), col, num_segments=N_NODES)
        has_nbr = counts > 0
        mean = sums / jnp.where(has_nbr, counts, 1.0)[:, None]
        out = jnp.where(has_nbr[:, None], mean, h)
        return out

    def _L1_gnn_ref(x, edge_index, edge_type, edge_emb_W, msg_W, msg_b, upd_W, upd_b, ln_g, ln_b):
        import jax, jax.numpy as jnp
        import numpy as np
        N, H = (6250, 128)
        E = 100000
        ETD = 32
        NUM_ET = 16
        LN_EPS = 1e-05
        src = edge_index[0]
        dst = edge_index[1]
        et = edge_emb_W[edge_type]
        m_in = jnp.concatenate([x[src], et], axis=-1)
        m = jax.nn.relu(m_in @ msg_W.T + msg_b)
        agg = jax.ops.segment_sum(m, dst, num_segments=x.shape[0])
        deg = jax.ops.segment_sum(jnp.ones_like(dst, dtype=x.dtype), dst, num_segments=x.shape[0])
        agg = agg / jnp.clip(deg, 1.0)[:, None]
        out = agg @ upd_W.T + upd_b
        h = x + out
        mu = jnp.mean(h, axis=-1, keepdims=True)
        var = jnp.mean((h - mu) ** 2, axis=-1, keepdims=True)
        return (h - mu) * jax.lax.rsqrt(var + LN_EPS) * ln_g + ln_b
    edge_index = jnp.stack([src, dst])
    h = jnp.maximum(_layernorm(x, axis=-1), 0.0)
    x = x + _L0_gnn_ref(h, edge_index, L0_gnn_W, L0_gnn_b)
    h = jnp.maximum(_layernorm(x, axis=-1), 0.0)
    x = x + _L1_gnn_ref(h, edge_index, edge_type_16, L1_gnn_edge_emb_W, L1_gnn_msg_W, L1_gnn_msg_b, L1_gnn_upd_W, L1_gnn_upd_b, L1_gnn_ln_g, L1_gnn_ln_b)
    return x

_drawn_inputs = setup_inputs


def setup_inputs(seed=0):
    import zlib

    import numpy as np

    out = dict(_drawn_inputs(seed))
    spreads = {'L1_gnn_ln_g': (1.0, 0.2), 'L1_gnn_ln_b': (0.0, 0.1)}
    factors = {'L1_gnn_msg_b': 3.593}
    for name, (base, spread) in spreads.items():
        noise = np.random.default_rng([zlib.crc32(name.encode()), seed]).standard_normal(out[name].shape)
        drawn = base * np.exp(spread * noise) if base else spread * noise
        out[name] = jnp.asarray(drawn.astype(out[name].dtype))
    for name, factor in factors.items():
        out[name] = (out[name] * factor).astype(out[name].dtype)
    return out
```

```python
from contextlib import ExitStack

import concourse.bass as bass
from concourse import mybir

P = 128
W = 64
TPG = 13
CH = (4, 3, 3, 3)
RING = 7
EPS = 1e-5

F32 = mybir.dt.float32
BF16 = mybir.dt.bfloat16
I32 = mybir.dt.int32
U32 = mybir.dt.uint32
ALU = mybir.AluOpType
ACT = mybir.ActivationFunctionType
AX = mybir.AxisListType
RMAX = bass.bass_isa.ReduceOp.max


def gnn_program(nc, x, idx_g, dst_t, dst_flat, gfirst, glast, types_g, w0t, b0, embt, wet, wxt, msgb,
                updt, updb, lng, lnb, consts, out, n_edges):
    N, D = x.shape
    TILES = -(-N // P)
    CHUNKS = TILES // RING
    GROUPS = idx_g.shape[0]
    PAIRS = GROUPS // 2
    NW = TILES * P // W
    NCOL = TILES * P + W
    LASTROWS = N - (TILES - 1) * P
    SLOT0 = [sum(CH[:c]) for c in range(len(CH))]
    NT = 16
    K3 = 3 * NT
    FR = (n_edges - 1) // P
    TAIL = n_edges - 1 - FR * P
    assert D == P and TILES % RING == 0 and GROUPS % 2 == 0 and sum(CH) == TPG and TAIL > 0

    with ExitStack() as ctx:
        def sb(name, shape, dt):
            return ctx.enter_context(nc.sbuf_tensor(name, shape, dt))

        def sem(name):
            return ctx.enter_context(nc.semaphore(name))

        table0 = nc.dram_tensor("table0", (TILES * P, D), F32, kind="Internal").ap()
        table1 = nc.dram_tensor("table1", (TILES * P, D), F32, kind="Internal").ap()

        xs = sb("xs", [P, TILES, D], F32)
        hs = sb("hs", [P, TILES, D], F32)
        accT = sb("accT", [P, NCOL], F32)
        cntT = sb("cntT", [P, NCOL], F32)
        gath = sb("gath", [P, 2, TPG, D], F32)
        msg = sb("msg", [P, TPG, D], F32)
        onehot = sb("onehot", [P, TPG, W], F32)
        typehot = sb("typehot", [K3, TPG, P], BF16)
        types = sb("types", [K3, 2, TPG * P], I32)
        idxb = sb("idxb", [P, 2, TPG], I32)
        dst_i = sb("dst_i", [P, GROUPS, TPG], I32)
        dst_r = sb("dst_r", [P, GROUPS, TPG], F32)
        dcur = sb("dcur", [P, TPG], F32)
        gfirst_i = sb("gfirst_i", [P, GROUPS], I32)
        glast_i = sb("glast_i", [1, GROUPS], I32)
        st_a = sb("st_a", [P, RING, D], F32)
        st_h = sb("st_h", [P, RING, D], F32)
        st_t = sb("st_t", [P, RING, D], F32)
        st_o = sb("st_o", [P, RING, D], F32)
        stats = sb("stats", [P, TILES, 6], F32)
        cstats = sb("cstats", [P, RING, 6], F32)
        small = sb("small", [P, 6, TILES], F32)
        rstd0 = sb("rstd0", [P, TILES], F32)
        nb0 = sb("nb0", [P, TILES], F32)
        csmall = sb("csmall", [P, 6, RING], F32)
        rstd1 = sb("rstd1", [P, RING], F32)
        nb1 = sb("nb1", [P, RING], F32)
        kc = sb("kc", [P, consts.shape[1]], F32)
        ones = sb("ones", [P, P], F32)
        w0 = sb("w0", [P, D], F32)
        wx = sb("wx", [P, D], F32)
        wu = sb("wu", [P, D], F32)
        emb_s = sb("emb_s", [embt.shape[0], K3], F32)
        wet_s = sb("wet_s", [wet.shape[0], D], F32)
        rows = sb("rows", [P, 5, D], F32)
        cmat = sb("cmat", [K3, 3, D], F32)
        cpart = sb("cpart", [K3, 3, D], BF16)
        csel = sb("csel", [K3, D], BF16)
        viol = sb("viol", [P, 8], F32)
        dmm = sb("dmm", [P, 4], F32)
        vmax = sb("vmax", [P, 2], F32)
        flag = sb("flag", [P, 1], I32)
        epsc = sb("epsc", [P, 1], F32)
        ends_i = sb("ends_i", [1, 2], I32)

        ident = kc[:, 0:P]
        iota = kc[:, P:P + W]
        tcol = kc[:, P + W:P + W + 1]
        b0r, msgbr, updbr, lngr, lnbr = (rows[:, k, :] for k in range(5))
        chk_a = gath[:, 0, :, :].rearrange("p t d -> p (t d)").bitcast(I32)[:, 0:FR]
        chk_b = gath[:, 1, :, :].rearrange("p t d -> p (t d)").bitcast(I32)[:, 0:FR]
        chk_d = msg[:, :, :].rearrange("p t d -> p (t d)")[:, 0:FR]
        tail_a = types[0:1, 0, 0:TAIL]
        tail_b = types[0:1, 1, 0:TAIL]
        tail_d = st_a[0:1, 0, 0:TAIL]

        ps = ctx.enter_context(nc.psum_tensor("ps", [P, 8, 512], F32))

        def slot(bank, j):
            return ps[:, bank + j // 4, (j % 4) * P:(j % 4 + 1) * P]

        def bank_full(j):
            return 4 if j < 4 else RING

        psA = ps[:, 6, 0:W]
        psN = ps[:, 7, 0:W]

        s_x = sem("s_x")
        s_in = sem("s_in")
        s_chk = sem("s_chk")
        s_pad = sem("s_pad")
        s_zero = sem("s_zero")
        s_dve = sem("s_dve")
        s_viol = sem("s_viol")
        s_vmax = sem("s_vmax")
        s_flag = sem("s_flag")
        s_dstr = sem("s_dstr")
        s_cps0 = sem("s_cps0")
        s_csel = sem("s_csel")
        s_var0 = sem("s_var0")
        s_std0 = sem("s_std0")
        s_nb0 = sem("s_nb0")
        s_h0 = sem("s_h0")
        s_tab = [sem(f"s_tab_l{l}") for l in range(2)]
        s_idx = [[sem(f"s_idx{l}{j}") for j in range(2)] for l in range(2)]
        s_gath = [[sem(f"s_gath{l}{j}") for j in range(2)] for l in range(2)]
        s_gfree = [sem(f"s_gfree{l}") for l in range(2)]
        s_typ = [sem(f"s_typ{j}") for j in range(2)]
        s_toh = sem("s_toh")
        s_cps = sem("s_cps")
        s_msg = sem("s_msg")
        s_relu = sem("s_relu")
        s_oh = [sem(f"s_oh{l}") for l in range(2)]
        s_agg = [sem(f"s_agg{l}") for l in range(2)]
        s_acc = [sem(f"s_acc_l{l}") for l in range(2)]
        s_rcnt = sem("s_rcnt")
        s_noedge = sem("s_noedge")
        s_hst = sem("s_hst")
        s_hnT = sem("s_hnT")
        s_st = [sem(f"s_st{l}") for l in range(2)]
        s_y = [sem(f"s_y{l}") for l in range(2)]
        s_x1 = [sem(f"s_x1_l{l}") for l in range(2)]
        s_var = [sem(f"s_var_l{l}") for l in range(2)]
        s_std = [sem(f"s_std_l{l}") for l in range(2)]
        s_nb = [sem(f"s_nb_l{l}") for l in range(2)]
        s_h1 = sem("s_h1")
        s_keep = sem("s_keep")
        s_hT = sem("s_hT")
        s_hTs = sem("s_hTs")
        s_p = sem("s_p")
        s_ps = sem("s_ps")
        s_acc0 = sem("s_acc0")
        s_z = sem("s_z")
        s_zg = sem("s_zg")
        s_fin = sem("s_fin")
        s_out = sem("s_out")
        s_bn0 = sem("s_bn0")
        s_bn = [sem(f"s_bn_l{l}") for l in range(2)]
        s_step = [sem(f"s_step{l}") for l in range(2)]
        s_dcur = [sem(f"s_dcur{l}") for l in range(2)]
        s_none = sem("s_none")
        s_apart = sem("s_apart")

        NIN = 16
        block = ctx.enter_context(nc.Block())

        def apart(eng):
            eng.sem_inc(s_apart, 1)

        def pairs(eng, body):
            for j in range(2):
                body(j, j, True)
            with eng.Fori(1, PAIRS) as i:
                for j in range(2):
                    body(i * 2 + j, j, False)

        def chunks(eng, body):
            body(0, True)
            with eng.Fori(1, CHUNKS) as c:
                body(c, False)

        @block.sync
        def _(sp):
            sp.wait_ge(s_pad, 1)
            sp.dma_start(xs[:, 0:TILES - 1, :],
                         x[0:(TILES - 1) * P, :].rearrange("(t p) d -> p t d", p=P)).then_inc(s_x, 16)
            sp.dma_start(xs[0:LASTROWS, TILES - 1, :], x[(TILES - 1) * P:N, :]).then_inc(s_x, 16)
            sp.dma_start(chk_a, dst_flat[0:FR * P].rearrange("(p n) -> p n", p=P)).then_inc(s_chk, 16)
            sp.dma_start(chk_b, dst_flat[1:FR * P + 1].rearrange("(p n) -> p n", p=P)).then_inc(s_chk, 16)
            sp.dma_start(tail_a, dst_flat[None, FR * P:n_edges - 1]).then_inc(s_chk, 16)
            sp.dma_start(tail_b, dst_flat[None, FR * P + 1:n_edges]).then_inc(s_chk, 16)
            sp.dma_start(ends_i[:, 0:1], dst_flat[None, 0:1]).then_inc(s_chk, 16)
            sp.dma_start(ends_i[:, 1:2], dst_flat[None, n_edges - 1:n_edges]).then_inc(s_chk, 16)
            loads = [(kc[:, :], consts), (w0[:, :], w0t), (wx[:, :], wxt), (wu[:, :], updt),
                     (wet_s[:, :], wet), (dst_i[:, :, :], dst_t), (gfirst_i[:, :], gfirst.to_broadcast([P, GROUPS])),
                     (glast_i[:, :], glast)]
            loads += [(emb_s[:, k * NT:(k + 1) * NT], embt) for k in range(3)]
            loads += [(r, v.to_broadcast([P, D])) for r, v in
                      zip((b0r, msgbr, updbr, lngr, lnbr), (b0, msgb, updb, lng, lnb))]
            assert len(loads) == NIN
            for to, of in loads:
                sp.dma_start(to, of).then_inc(s_in, 16)

            sp.wait_ge(s_h0, TILES)
            sp.dma_start(table0.rearrange("(t p) d -> p t d", p=P), hs[:, :, :]).then_inc(s_tab[0], 16)

            def load_edges(l, n, j, first):
                if not first:
                    sp.wait_ge(s_gath[l][j], (n - j) * (8 * TPG))
                sp.dma_start(idxb[:, j, :], idx_g[n]).then_inc(s_idx[l][j], 16)
                if l:
                    if not first:
                        sp.wait_ge(s_toh, n - 1)
                    sp.dma_start(types[:, j, :], types_g[n].to_broadcast([K3, TPG * P])).then_inc(s_typ[j], 16)

            pairs(sp, lambda n, j, first: load_edges(0, n, j, first))
            t1 = table1.rearrange("(c j p) d -> c p j d", j=RING, p=P)
            with sp.Fori(0, CHUNKS) as c:
                sp.wait_ge(s_ps, (c + 1) * RING)
                sp.dma_start(t1[c], st_o[:, :, :]).then_inc(s_tab[1], 16)
            pairs(sp, lambda n, j, first: load_edges(1, n, j, first))

            oc = out[0:(CHUNKS - 1) * RING * P, :].rearrange("(c j p) d -> c p j d", j=RING, p=P)
            with sp.Fori(0, CHUNKS - 1) as c:
                sp.wait_ge(s_fin, (c + 1) * RING)
                sp.dma_start(oc[c], st_o[:, :, :]).then_inc(s_out, 16)
            sp.wait_ge(s_fin, TILES)
            at = (CHUNKS - 1) * RING * P
            sp.dma_start(out[at:at + (RING - 1) * P, :].rearrange("(j p) d -> p j d", p=P),
                         st_o[:, 0:RING - 1, :]).then_inc(s_out, 16)
            sp.dma_start(out[(TILES - 1) * P:N, :], st_o[0:LASTROWS, RING - 1, :]).then_inc(s_out, 16)
            sp.wait_ge(s_out, (CHUNKS + 1) * 16)

        @block.gpsimd
        def _(pool):
            nc.gpsimd.memset(xs[:, TILES - 1, :], 0.0).then_inc(s_pad, 1)
            nc.gpsimd.memset(accT[:, :], 0.0).then_inc(s_acc[0], 1)
            nc.gpsimd.memset(cntT[:, :], 0.0).then_inc(s_zero, 1)
            nc.gpsimd.memset(ones[:, :], 1.0).then_inc(s_zero, 1)
            pool.wait_ge(s_viol, 1)
            nc.gpsimd.partition_all_reduce(vmax[:, 1:2], vmax[:, 0:1], P, RMAX).then_inc(s_vmax, 1)

            def gather(l, n, j, first):
                table = (table0, table1)[l]
                pool.wait_ge(s_idx[l][j], (n - j) * 8 + 16)
                if not first:
                    if l:
                        pool.wait_ge(s_msg, (n - 1) * len(CH))
                    else:
                        pool.wait_ge(s_gfree[0], n - 1)
                apart(pool)
                for k in range(TPG):
                    pool.indirect_dma_start(
                        gath[:, j, k, :], None, table,
                        bass.IndirectOffsetOnAxis(ap=idxb[:, j, k:k + 1].bitcast(U32), axis=0),
                    ).then_inc(s_gath[l][j], 16)

            pool.wait_ge(s_tab[0], 16)
            pool.wait_ge(s_flag, 1)
            pairs(pool, lambda n, j, first: gather(0, n, j, first))

            with pool.Fori(0, CHUNKS) as c:
                for j in range(RING):
                    pool.wait_ge(s_h1, c * RING + (j + 1))
                    nc.gpsimd.tensor_tensor(hs[:, bass.ds(c * RING + j, 1), :], st_h[:, j:j + 1, :],
                                            rows[:, 2:3, :], ALU.add).then_inc(s_keep, 1)
                    nc.gpsimd.tensor_tensor(xs[:, bass.ds(c * RING + j, 1), :], xs[:, bass.ds(c * RING + j, 1), :],
                                            rows[:, 4:5, :], ALU.add).then_inc(s_keep, 1)
            pool.wait_ge(s_tab[1], 16 * CHUNKS)
            pairs(pool, lambda n, j, first: gather(1, n, j, first))

            def finish_rows(c, first):
                for j in range(RING):
                    pool.wait_ge(s_z, c * RING + (j + 1))
                    nc.gpsimd.tensor_tensor(st_t[:, j:j + 1, :], st_h[:, j:j + 1, :],
                                            rows[:, 3:4, :], ALU.mult).then_inc(s_zg, 1)
                    if j == 0:
                        if not first:
                            pool.wait_ge(s_out, c * 16)
                    pool.wait_ge(s_zg, c * RING + (j + 1))
                    nc.gpsimd.tensor_tensor(st_o[:, j:j + 1, :], st_t[:, j:j + 1, :],
                                            xs[:, bass.ds(c * RING + j, 1), :], ALU.add).then_inc(s_fin, 1)

            chunks(pool, finish_rows)

        @block.scalar
        def _(act):
            act.wait_ge(s_var0, 1)
            nc.scalar.activation(small[:, 5, :], small[:, 4, :], ACT.Sqrt, bias=epsc[:, 0:1],
                                 scale=1.0 / D).then_inc(s_std0, 1)
            act.wait_ge(s_nb0, 1)
            with act.Fori(0, CHUNKS) as c:
                for j in range(RING):
                    t = c * RING + j
                    nc.scalar.activation(hs[:, t, :], xs[:, t, :], ACT.Relu, bias=nb0[:, bass.ds(t, 1)],
                                         scale=rstd0[:, bass.ds(t, 1)]).then_inc(s_h0, 1)

            def table_rows(c, first):
                act.wait_ge(s_var[0], c + 1)
                nc.scalar.activation(csmall[:, 5, :], csmall[:, 4, :], ACT.Sqrt, bias=epsc[:, 0:1],
                                     scale=1.0 / D).then_inc(s_std[0], 1)
                act.wait_ge(s_nb[0], c + 1)
                if not first:
                    act.wait_ge(s_keep, c * (2 * RING))
                if not first:
                    act.wait_ge(s_hT, c * RING)
                for j in range(RING):
                    nc.scalar.activation(st_h[:, j, :], xs[:, c * RING + j, :], ACT.Relu, bias=nb1[:, j:j + 1],
                                         scale=rstd1[:, j:j + 1]).then_inc(s_h1, 1)
                for j in range(RING):
                    act.wait_ge(s_hT, c * RING + bank_full(j))
                    nc.scalar.activation(st_t[:, j, :], slot(2, j), ACT.Copy).then_inc(s_hTs, 1)
                if not first:
                    act.wait_ge(s_tab[1], c * 16)
                for j in range(RING):
                    act.wait_ge(s_p, c * RING + bank_full(j))
                    nc.scalar.activation(st_o[:, j, :], slot(4, j), ACT.Copy).then_inc(s_ps, 1)

            chunks(act, table_rows)

            def relu_messages(n, j, first):
                for c, w in enumerate(CH):
                    act.wait_ge(s_msg, n * len(CH) + (c + 1))
                    m = msg[:, SLOT0[c]:SLOT0[c] + w, :]
                    nc.scalar.activation(m, m, ACT.Relu).then_inc(s_relu, 1)

            pairs(act, relu_messages)

            def normalise(c, first):
                act.wait_ge(s_var[1], c + 1)
                nc.scalar.activation(csmall[:, 5, :], csmall[:, 4, :], ACT.Sqrt, bias=epsc[:, 0:1],
                                     scale=1.0 / D).then_inc(s_std[1], 1)
                act.wait_ge(s_nb[1], c + 1)
                if not first:
                    act.wait_ge(s_zg, c * RING)
                for j in range(RING):
                    nc.scalar.activation(st_h[:, j, :], hs[:, c * RING + j, :], ACT.Identity, bias=nb1[:, j:j + 1],
                                         scale=rstd1[:, j:j + 1]).then_inc(s_z, 1)

            chunks(act, normalise)

        @block.tensor
        def _(pe):
            pe.wait_ge(s_in, 16 * NIN)
            nc.tensor.matmul(slot(0, 0)[0:K3, :], emb_s[:, :], wet_s[:, :], start=True, stop=True).then_inc(s_cps0, 1)
            pe.wait_ge(s_zero, 2)
            pe.wait_ge(s_flag, 1)
            flag_pe = pe.value_load(flag[0:1, 0:1], min_val=0, max_val=1)

            def type_terms(n, first):
                pe.wait_ge(s_toh, n + 1)
                if not first:
                    pe.wait_ge(s_msg, n * len(CH))
                for c, w in enumerate(CH):
                    for k in range(w):
                        last = nc.tensor.matmul(ps[:, c, k * P:(k + 1) * P], typehot[:, SLOT0[c] + k, :],
                                                csel[:, :], start=True, stop=True)
                    last.then_inc(s_cps, 1)

            def window_sums(l, n, j, q):
                rows_of = (gath[:, j], msg)[l]
                pe.wait_ge(s_oh[l], q + 1)
                for k in range(TPG):
                    if l and k in SLOT0:
                        pe.wait_ge(s_relu, n * len(CH) + (SLOT0.index(k) + 1))
                    last = nc.tensor.matmul(psA, rows_of[:, k, :], onehot[:, k, :], start=(k == 0), stop=(k == TPG - 1))
                if l == 0:
                    for k in range(TPG):
                        last = nc.tensor.matmul(psN, ones[:, :], onehot[:, k, :], start=(k == 0), stop=(k == TPG - 1))
                last.then_inc(s_agg[l], 1)

            def layer(l):
                def group(n, j, first, windows):
                    if l:
                        type_terms(n, first and j == 0)
                    else:
                        pe.wait_ge(s_gath[0][j], (n - j) * (8 * TPG) + 16 * TPG)
                    if windows:
                        apart(pe)
                        with pe.Fori(0, NW) as w:
                            window_sums(l, n, j, n * NW + w)
                    else:
                        window_sums(l, n, j, n)

                def no_edges(t):
                    pe.wait_ge(s_hst, t + 1)
                    nc.tensor.transpose(slot(0, 0), st_h[:, 0, :], ident).then_inc(s_hnT, 1)

                with pe.If(flag_pe == 0):
                    pairs(pe, lambda n, j, first: group(n, j, first, False))
                with pe.Else():
                    pairs(pe, lambda n, j, first: group(n, j, first, True))
                    if l == 0:
                        with pe.Fori(0, TILES) as t:
                            no_edges(t)

            layer(0)
            def node_products(c, first):
                if not first:
                    pe.wait_ge(s_x1[0], c * RING)
                for j in range(RING):
                    pe.wait_ge(s_st[0], c * RING + (j + 1))
                    nc.tensor.matmul(slot(0, j), st_a[:, j, :], w0[:, :], start=True, stop=True).then_inc(s_y[0], 1)
                if not first:
                    pe.wait_ge(s_hTs, c * RING)
                for j in range(RING):
                    pe.wait_ge(s_h1, c * RING + (j + 1))
                    nc.tensor.transpose(slot(2, j), st_h[:, j, :], ident).then_inc(s_hT, 1)
                if not first:
                    pe.wait_ge(s_ps, c * RING)
                for j in range(RING):
                    pe.wait_ge(s_hTs, c * RING + (j + 1))
                    nc.tensor.matmul(slot(4, j), st_t[:, j, :], wx[:, :], start=True, stop=True).then_inc(s_p, 1)

            chunks(pe, node_products)
            layer(1)
            def update_products(c, first):
                if not first:
                    pe.wait_ge(s_x1[1], c * RING)
                for j in range(RING):
                    pe.wait_ge(s_st[1], c * RING + (j + 1))
                    nc.tensor.matmul(slot(0, j), st_a[:, j, :], wu[:, :], start=True, stop=True).then_inc(s_y[1], 1)

            chunks(pe, update_products)

        @block.vector
        def _(dve):
            chained = [0]

            def chain(ins):
                chained[0] += 1
                ins.then_inc(s_dve, 1)
                dve.wait_ge(s_dve, chained[0])

            def spread(st, sm, step):
                me, qe, mo, qo = (st[:, :, k] for k in (1, 2, 4, 5))
                step(nc.vector.tensor_tensor(sm[:, 0, :], me, mo, ALU.add))
                step(nc.vector.tensor_tensor(sm[:, 1, :], me, mo, ALU.subtract))
                step(nc.vector.tensor_tensor(sm[:, 2, :], qe, qo, ALU.add))
                step(nc.vector.tensor_tensor(sm[:, 3, :], sm[:, 1, :], sm[:, 1, :], ALU.mult))
                return nc.vector.scalar_tensor_tensor(sm[:, 4, :], sm[:, 3, :], D / 4.0, sm[:, 2, :],
                                                      ALU.mult, ALU.add)

            nc.vector.memset(epsc[:, :], EPS)
            chain(nc.vector.memset(viol[:, :], 0.0))
            dve.wait_ge(s_x, 32)
            with dve.Fori(0, CHUNKS) as c:
                for j in range(RING):
                    nc.vector.bn_stats(stats[:, c * RING + j, :], xs[:, c * RING + j, :]).then_inc(s_bn0, 1)
            dve.wait_ge(s_bn0, TILES)
            spread(stats, small, chain).then_inc(s_var0, 1)
            dve.wait_ge(s_std0, 1)
            chain(nc.vector.reciprocal(rstd0[:, :], small[:, 5, :]))
            nc.vector.scalar_tensor_tensor(nb0[:, :], small[:, 0, :], -0.5, rstd0[:, :],
                                           ALU.mult, ALU.mult).then_inc(s_nb0, 1)

            dve.wait_ge(s_chk, 16 * 6)
            dve.wait_ge(s_in, 16 * NIN)
            chain(nc.vector.tensor_tensor(chk_d, chk_b, chk_a, ALU.subtract))
            chain(nc.vector.tensor_tensor(tail_d, tail_b, tail_a, ALU.subtract))
            chain(nc.vector.tensor_reduce(dmm[:, 0:1], chk_d, AX.X, ALU.max))
            chain(nc.vector.tensor_reduce(dmm[:, 1:2], chk_d, AX.X, ALU.min))
            chain(nc.vector.tensor_reduce(dmm[0:1, 2:3], tail_d, AX.X, ALU.max))
            chain(nc.vector.tensor_reduce(dmm[0:1, 3:4], tail_d, AX.X, ALU.min))
            chain(nc.vector.tensor_scalar(viol[:, 0:1], dmm[:, 0:1], -1.0, None, ALU.add))
            chain(nc.vector.tensor_scalar(viol[:, 1:2], dmm[:, 1:2], -1.0, None, ALU.mult))
            chain(nc.vector.tensor_scalar(viol[0:1, 2:3], dmm[0:1, 2:3], -1.0, None, ALU.add))
            chain(nc.vector.tensor_scalar(viol[0:1, 3:4], dmm[0:1, 3:4], -1.0, None, ALU.mult))
            chain(nc.vector.tensor_copy(viol[0:1, 4:5], ends_i[0:1, 0:1]))
            chain(nc.vector.tensor_scalar(viol[0:1, 5:6], ends_i[0:1, 1:2], -1.0, float(N - 1), ALU.mult, ALU.add))
            span = st_a[0:1, 1, 0:GROUPS]
            chain(nc.vector.tensor_tensor(span, glast_i[0:1, :], gfirst_i[0:1, :], ALU.subtract))
            chain(nc.vector.tensor_reduce(viol[0:1, 6:7], span, AX.X, ALU.max))
            chain(nc.vector.tensor_scalar(viol[0:1, 6:7], viol[0:1, 6:7], -float(W - 1), None, ALU.add))
            nc.vector.tensor_reduce(vmax[:, 0:1], viol[:, :], AX.X, ALU.max).then_inc(s_viol, 1)
            dve.wait_ge(s_vmax, 1)
            nc.vector.tensor_scalar(flag[:, :], vmax[:, 1:2], 0.0, None, ALU.is_gt).then_inc(s_flag, 1)
            one_window = dmm[:, 0:1]
            chain(nc.vector.tensor_scalar(one_window, vmax[:, 1:2], 0.0, None, ALU.is_le))
            base = st_a[:, 2, 0:GROUPS]
            chain(nc.vector.tensor_scalar(base, gfirst_i[:, :], one_window, None, ALU.mult))
            chain(nc.vector.tensor_tensor(dst_r[:, :, :], dst_i[:, :, :],
                                          base[:, :, None].to_broadcast([P, GROUPS, TPG]), ALU.subtract))

            dve.wait_ge(s_cps0, 1)
            chain(nc.vector.tensor_tensor(cmat[:, 0, :], slot(0, 0)[0:K3, :], msgbr[0:K3, :], ALU.add))
            chain(nc.vector.tensor_copy(cpart[:, 0, :], cmat[:, 0, :]))
            chain(nc.vector.tensor_tensor(cmat[:, 1, :], cmat[:, 0, :], cpart[:, 0, :], ALU.subtract))
            chain(nc.vector.tensor_copy(cpart[:, 1, :], cmat[:, 1, :]))
            chain(nc.vector.tensor_tensor(cmat[:, 2, :], cmat[:, 1, :], cpart[:, 1, :], ALU.subtract))
            chain(nc.vector.tensor_copy(cpart[:, 2, :], cmat[:, 2, :]))
            third = [kc[0:K3, P + W + 1 + k:P + W + 2 + k] for k in range(3)]
            chain(nc.vector.tensor_scalar(cmat[:, 0, :], cpart[:, 0, :], third[0], None, ALU.mult))
            chain(nc.vector.scalar_tensor_tensor(cmat[:, 1, :], cpart[:, 1, :], third[1], cmat[:, 0, :],
                                                 ALU.mult, ALU.add))
            nc.vector.scalar_tensor_tensor(csel[:, :], cpart[:, 2, :], third[2], cmat[:, 1, :],
                                           ALU.mult, ALU.add).then_inc(s_csel, 1)

            dve.wait_ge(s_h0, TILES)
            chain(nc.vector.tensor_tensor(xs[:, :, :], xs[:, :, :],
                                          rows[:, 0:1, :].to_broadcast([P, TILES, D]), ALU.add))
            dve.wait_ge(s_zero, 2)
            flag_dve = dve.value_load(flag[0:1, 0:1], min_val=0, max_val=1)

            def make_onehot(l, q, dst):
                dve.wait_ge(s_acc[l], q * (2 - l) + 1)
                nc.vector.tensor_tensor(onehot[:, :, :], kc[:, None, P:P + W].to_broadcast([P, TPG, W]),
                                        dst[:, :, None].to_broadcast([P, TPG, W]), ALU.is_equal).then_inc(s_oh[l], 1)

            def add_window(l, q, col):
                dve.wait_ge(s_agg[l], q + 1)
                nc.vector.tensor_tensor(accT[:, bass.ds(col, W)], accT[:, bass.ds(col, W)], psA,
                                        ALU.add).then_inc(s_acc[l], 1)
                if l == 0:
                    nc.vector.tensor_tensor(cntT[:, bass.ds(col, W)], cntT[:, bass.ds(col, W)], psN,
                                            ALU.add).then_inc(s_acc[l], 1)

            def messages(n, j):
                dve.wait_ge(s_typ[j], (n - j) * 8 + 16)
                nc.vector.tensor_scalar(typehot[:, :, :].rearrange("k t e -> k (t e)"), types[:, j, :],
                                        kc[0:K3, P + W:P + W + 1], None, ALU.is_equal).then_inc(s_toh, 1)
                dve.wait_ge(s_gath[1][j], (n - j) * (8 * TPG) + 16 * TPG)
                for c, w in enumerate(CH):
                    dve.wait_ge(s_cps, n * len(CH) + (c + 1))
                    nc.vector.tensor_tensor(msg[:, SLOT0[c]:SLOT0[c] + w, :], gath[:, j, SLOT0[c]:SLOT0[c] + w, :],
                                            ps[:, c, 0:w * P].rearrange("p (t d) -> p t d", d=D),
                                            ALU.add).then_inc(s_msg, 1)

            def layer(l):
                def group(n, j, first):
                    make_onehot(l, n, dst_r[:, n, :])
                    if l:
                        messages(n, j)
                    col = dve.value_load(gfirst_i[0:1, bass.ds(n, 1)], min_val=0, max_val=N - 1)
                    add_window(l, n, col)
                    if l == 0:
                        dve.sem_inc(s_gfree[0], 1)

                def group_all_windows(n, j, first):
                    if l:
                        messages(n, j)
                    nc.vector.tensor_copy(dcur[:, :], dst_r[:, n, :]).then_inc(s_dcur[l], 1)
                    with dve.Fori(0, NW) as w:
                        q = n * NW + w
                        dve.wait_ge(s_dcur[l], n * (NW + 1) + w + 1)
                        make_onehot(l, q, dcur)
                        dve.wait_ge(s_oh[l], q + 1)
                        nc.vector.tensor_scalar(dcur[:, :], dcur[:, :], -float(W), None, ALU.add).then_inc(s_dcur[l], 1)
                        add_window(l, q, w * W)
                    if l == 0:
                        dve.sem_inc(s_gfree[0], 1)

                def no_edges(t):
                    col = bass.ds(t * P, P)
                    nc.vector.tensor_copy(st_h[:, 0, :], hs[:, t, :]).then_inc(s_hst, 1)
                    nc.vector.tensor_scalar(st_a[:, 0, :], cntT[:, col], 0.0, None, ALU.is_equal).then_inc(s_none, 1)
                    dve.wait_ge(s_hnT, t + 1)
                    dve.wait_ge(s_none, t * 3 + 1)
                    nc.vector.tensor_tensor(st_t[:, 0, :], st_a[:, 0, :], slot(0, 0), ALU.mult).then_inc(s_none, 1)
                    dve.wait_ge(s_none, t * 3 + 2)
                    nc.vector.tensor_tensor(accT[:, col], accT[:, col], st_t[:, 0, :], ALU.add).then_inc(s_none, 1)
                    dve.wait_ge(s_none, t * 3 + 3)

                with dve.If(flag_dve == 0):
                    pairs(dve, group)
                    dve.wait_ge(s_acc[l], GROUPS * (2 - l) + 1)
                with dve.Else():
                    pairs(dve, group_all_windows)
                    dve.wait_ge(s_acc[l], GROUPS * NW * (2 - l) + 1)
                    if l == 0:
                        with dve.Fori(0, TILES) as t:
                            no_edges(t)

            def nodes(l, c, first):
                steps = [0]

                def step(ins):
                    steps[0] += 1
                    ins.then_inc(s_step[l], 1)
                    dve.wait_ge(s_step[l], c * 5 + steps[0])

                for j in range(RING):
                    col = bass.ds((c * RING + j) * P, P)
                    nc.vector.tensor_tensor(st_a[:, j, :], accT[:, col], cntT[:, col], ALU.mult).then_inc(s_st[l], 1)
                keep = (xs, hs)[l]
                for j in range(RING):
                    t = c * RING + j
                    dve.wait_ge(s_y[l], c * RING + bank_full(j))
                    nc.vector.tensor_tensor(keep[:, t, :], slot(0, j), keep[:, t, :], ALU.add).then_inc(s_x1[l], 1)
                dve.wait_ge(s_x1[l], c * RING + RING)
                apart(dve)
                for j in range(RING):
                    nc.vector.bn_stats(cstats[:, j, :], keep[:, c * RING + j, :]).then_inc(s_bn[l], 1)
                dve.wait_ge(s_bn[l], c * RING + RING)
                spread(cstats, csmall, step).then_inc(s_var[l], 1)
                dve.wait_ge(s_std[l], c + 1)
                if not first:
                    dve.wait_ge((s_h1, s_z)[l], c * RING)
                step(nc.vector.reciprocal(rstd1[:, :], csmall[:, 5, :]))
                nc.vector.scalar_tensor_tensor(nb1[:, :], csmall[:, 0, :], -0.5, rstd1[:, :],
                                               ALU.mult, ALU.mult).then_inc(s_nb[l], 1)

            layer(0)
            chain(nc.vector.tensor_scalar(cntT[:, :], cntT[:, :], 1.0, None, ALU.max))
            chain(nc.vector.reciprocal(cntT[:, :], cntT[:, :]))
            chunks(dve, lambda c, first: nodes(0, c, first))
            dve.wait_ge(s_st[0], TILES)
            nc.vector.memset(accT[:, :], 0.0).then_inc(s_acc[1], 1)
            layer(1)
            dve.wait_ge(s_keep, 2 * TILES)
            chunks(dve, lambda c, first: nodes(1, c, first))


def kernel(x, src, dst, edge_type_16, L0_gnn_W, L0_gnn_b, L1_gnn_edge_emb_W, L1_gnn_msg_W, L1_gnn_msg_b,
           L1_gnn_upd_W, L1_gnn_upd_b, L1_gnn_ln_g, L1_gnn_ln_b):
    import numpy as np
    import concourse.bacc as bacc
    from concourse.bass_utils import run_bass_kernel_spmd

    x, src, dst, typ = (np.asarray(a) for a in (x, src, dst, edge_type_16))
    N, D = x.shape
    E = src.shape[0]
    per = TPG * P
    groups = -(-E // per)
    groups += groups % 2
    pad = groups * per - E

    def padded(a, value):
        return np.concatenate([a, np.full((pad,), value, a.dtype)])

    src_p, dst_p, typ_p = padded(src, 0), padded(dst, 1 << 20), padded(typ, 0)
    first = np.minimum(np.arange(groups) * per, E - 1)
    last = np.minimum(first + per, E) - 1
    consts = np.zeros((P, P + W + 4), np.float32)
    consts[:, 0:P] = np.eye(P)
    consts[:, P:P + W] = np.arange(W)
    consts[:, P + W] = np.arange(P) % 16
    for k in range(3):
        consts[16 * k:16 * k + 16, P + W + 1 + k] = 1.0
    row = lambda a: np.asarray(a).reshape(1, -1)
    cols = lambda a: np.ascontiguousarray(np.asarray(a).T)
    msg_w = np.asarray(L1_gnn_msg_W)
    arrays = {
        "x": x,
        "idx_g": np.ascontiguousarray(src_p.reshape(groups, TPG, P).transpose(0, 2, 1)),
        "dst_t": np.ascontiguousarray(dst_p.reshape(groups, TPG, P).transpose(2, 0, 1)),
        "dst_flat": dst,
        "gfirst": row(dst[first]),
        "glast": row(dst[last]),
        "types_g": typ_p.reshape(groups, 1, per),
        "w0t": cols(L0_gnn_W),
        "b0": row(L0_gnn_b),
        "embt": cols(L1_gnn_edge_emb_W),
        "wet": cols(msg_w[:, D:]),
        "wxt": cols(msg_w[:, :D]),
        "msgb": row(L1_gnn_msg_b),
        "updt": cols(L1_gnn_upd_W),
        "updb": row(L1_gnn_upd_b),
        "lng": row(L1_gnn_ln_g),
        "lnb": row(L1_gnn_ln_b),
        "consts": consts,
    }
    nc = bacc.Bacc("TRN2", target_bir_lowering=False, num_devices=1)
    args = [nc.dram_tensor(k, a.shape, mybir.dt.from_np(a.dtype), kind="ExternalInput").ap()
            for k, a in arrays.items()]
    out = nc.dram_tensor("out", (N, D), F32, kind="ExternalOutput").ap()
    gnn_program(nc, *args, out, E)
    r = run_bass_kernel_spmd(nc, [arrays], core_ids=[0])
    return r.results[0]["out"]
```

```python
from contextlib import ExitStack

import concourse.bass as bass
from concourse import mybir

P = 128
W = 64
TPG = 13
CH = (4, 3, 3, 3)
WT = 7
TPB = 18
WB = 96
SCALE = 4096.0
RING = 7
EPS = 1e-5

F32 = mybir.dt.float32
BF16 = mybir.dt.bfloat16
F16 = mybir.dt.float16
I32 = mybir.dt.int32
U32 = mybir.dt.uint32
ALU = mybir.AluOpType
ACT = mybir.ActivationFunctionType
AX = mybir.AxisListType
RMAX = bass.bass_isa.ReduceOp.max


def gnn_program(nc, x, idx_g, src_t, dst_t, dst_flat, tfirst, tlast, bfirst, blast, trep, gfirst, glast, types_g, w0t, b0, embt, wet, wxt, msgb,
                updt, updb, lng, lnb, consts, out, n_edges):
    N, D = x.shape
    TILES = -(-N // P)
    CHUNKS = TILES // RING
    GROUPS = idx_g.shape[0]
    PAIRS = GROUPS // 2
    NW = TILES * P // W
    NCOL = TILES * P + WB
    LASTROWS = N - (TILES - 1) * P
    SLOT0 = [sum(CH[:c]) for c in range(len(CH))]
    NT = 16
    K3 = 3 * NT
    FR = (n_edges - 1) // P
    TAIL = n_edges - 1 - FR * P
    ALLT = src_t.shape[1]
    BLOCKS = ALLT // TPB - 1
    ROWS = TPB * WT
    ZC = TILES * WT
    ZP = ZC + (-ZC) % 4
    NIOTA = consts.shape[1] - P - 5
    assert BLOCKS % 2 == 0 and BLOCKS >= 4 and ZP <= 512 and ROWS <= P and NIOTA >= max(ZP, P, WB)
    assert D == P and TILES % RING == 0 and GROUPS % 2 == 0 and sum(CH) == TPG and TAIL > 0

    with ExitStack() as ctx:
        def sb(name, shape, dt):
            return ctx.enter_context(nc.sbuf_tensor(name, shape, dt))

        def sem(name):
            return ctx.enter_context(nc.semaphore(name))

        table0 = nc.dram_tensor("table0", (TILES * P, D), F32, kind="Internal").ap()
        table1 = nc.dram_tensor("table1", (TILES * P, D), F32, kind="Internal").ap()

        xs = sb("xs", [P, TILES, D], F32)
        hs = sb("hs", [P, TILES, D], F32)
        accT = sb("accT", [P, NCOL], F32)
        cntT = sb("cntT", [P, NCOL], F32)
        WORDS = max((TPB * (ZP + P) + 2 * TILES * ROWS) // 2, 3 * TPG * D + TPG * W + TPG * P // 2 + 2 * TPG * P)
        work = sb("work", [P, WORDS], F32)
        used = [0]

        def carve(words):
            used[0] += words
            return work[:, used[0] - words:used[0]]

        zhot = carve(TPB * ZP // 2).bitcast(F16).rearrange("p (t z) -> p t z", t=TPB)
        lohot = carve(TPB * P // 2).bitcast(F16).rearrange("p (t l) -> p t l", t=TPB)
        adj = carve(TILES * ROWS).bitcast(F16).rearrange("p (j h r) -> p j h r", j=2, h=TILES)
        used[0] = 0
        gath = carve(2 * TPG * D).rearrange("p (j t d) -> p j t d", j=2, t=TPG)
        msg = carve(TPG * D).rearrange("p (t d) -> p t d", t=TPG)
        onehot = carve(TPG * W).rearrange("p (t w) -> p t w", t=TPG)
        typehot = carve(TPG * P // 2)[0:K3].bitcast(BF16).rearrange("p (t e) -> p t e", t=TPG)
        types = carve(2 * TPG * P)[0:K3].bitcast(I32).rearrange("p (j e) -> p j e", j=2)
        idxb = sb("idxb", [P, 2, TPG], I32)
        dst_i = sb("dst_i", [P, ALLT], I32)
        code = dst_i[:, :].bitcast(F32)
        src_lo = sb("src_lo", [P, ALLT], F32)
        cols = sb("cols", [P, 2, 2, TPB], F32)
        h_hi = sb("h_hi", [P, TILES, D + 1], F16)
        h_lo = sb("h_lo", [P, TILES, D], F16)
        st = h_lo[:, :, :].rearrange("p t d -> p (t d)").bitcast(F32)[:, 0:3 * RING * D]
        st_a, st_h, st_t = (st.rearrange("p (k j d) -> p k j d", k=3, j=RING)[:, k] for k in range(3))
        iota16 = sb("iota16", [P, ZP], F16)
        sums = sb("sums", [ROWS, D + 1], F32)
        place = sb("place", [ROWS, 2, WB], F32)
        vrow = sb("vrow", [ROWS, BLOCKS + 1], F32)
        bfirst_i = sb("bfirst_i", [P, BLOCKS + 1], I32)
        dst_r = sb("dst_r", [P, GROUPS, TPG], F32)
        dcur = sb("dcur", [P, TPG], F32)
        gfirst_i = sb("gfirst_i", [P, GROUPS], I32)
        glast_i = sb("glast_i", [1, GROUPS], I32)
        st_o = sb("st_o", [P, RING, D], F32)
        stats = sb("stats", [P, TILES, 6], F32)
        cstats = sb("cstats", [P, RING, 6], F32)
        small = sb("small", [P, 6, TILES], F32)
        rstd0 = sb("rstd0", [P, TILES], F32)
        nb0 = sb("nb0", [P, TILES], F32)
        csmall = sb("csmall", [P, 6, RING], F32)
        rstd1 = sb("rstd1", [P, RING], F32)
        nb1 = sb("nb1", [P, RING], F32)
        kc = sb("kc", [P, consts.shape[1]], F32)
        ones = sb("ones", [P, P], F32)
        w0 = sb("w0", [P, D], F32)
        wx = sb("wx", [P, D], F32)
        wu = sb("wu", [P, D], F32)
        emb_s = sb("emb_s", [embt.shape[0], K3], F32)
        wet_s = sb("wet_s", [wet.shape[0], D], F32)
        rows = sb("rows", [P, 5, D], F32)
        cmat = sb("cmat", [K3, 3, D], F32)
        cpart = sb("cpart", [K3, 3, D], BF16)
        csel = sb("csel", [K3, D], BF16)
        viol = sb("viol", [P, 9], F32)
        dmm = sb("dmm", [P, 4], F32)
        vmax = sb("vmax", [P, 2], F32)
        flag = sb("flag", [P, 1], I32)
        epsc = sb("epsc", [P, 1], F32)
        ends_i = sb("ends_i", [1, 2], I32)

        ident = kc[:, 0:P]
        KI = P + NIOTA
        b0r, msgbr, updbr, lngr, lnbr = (rows[:, k, :] for k in range(5))
        used[0] = 0
        chk_a_all = carve(ALLT).bitcast(I32)
        chk_a = chk_a_all[:, 0:FR]
        chk_b = carve(ALLT).bitcast(I32)[:, 0:FR]
        spans = carve(ALLT)
        chk_d = spans[:, 0:FR]
        src_i = carve(ALLT).bitcast(I32)
        tfirst_i = carve(ALLT).bitcast(I32)
        tlast_i = carve(ALLT).bitcast(I32)[0:1, :]
        tail = carve(3 * TAIL)
        tail_a, tail_b = (tail[0:1, k * TAIL:(k + 1) * TAIL].bitcast(I32) for k in range(2))
        tail_d = tail[0:1, 2 * TAIL:3 * TAIL]
        blast_i = carve(BLOCKS + 1).bitcast(I32)[0:1, :]
        trep_i = carve(BLOCKS + 1).bitcast(I32)[0:ROWS, :]
        assert used[0] <= WORDS

        ps = ctx.enter_context(nc.psum_tensor("ps", [P, 8, 512], F32))

        def slot(bank, j):
            return ps[:, bank + j // 4, (j % 4) * P:(j % 4 + 1) * P]

        def bank_full(j):
            return 4 if j < 4 else RING

        psA = ps[:, 6, 0:W]
        psN = ps[:, 7, 0:W]

        s_x = sem("s_x")
        s_in = sem("s_in")
        s_chk = sem("s_chk")
        s_pad = sem("s_pad")
        s_zero = sem("s_zero")
        s_dve = sem("s_dve")
        s_viol = sem("s_viol")
        s_vmax = sem("s_vmax")
        s_flag = sem("s_flag")
        s_dstr = sem("s_dstr")
        s_cps0 = sem("s_cps0")
        s_csel = sem("s_csel")
        s_var0 = sem("s_var0")
        s_std0 = sem("s_std0")
        s_nb0 = sem("s_nb0")
        s_h0 = sem("s_h0")
        s_tab = [sem(f"s_tab_l{l}") for l in range(2)]
        s_idx = [[sem(f"s_idx{l}{j}") for j in range(2)] for l in range(2)]
        s_gath = [[sem(f"s_gath{l}{j}") for j in range(2)] for l in range(2)]
        s_gfree = [sem(f"s_gfree{l}") for l in range(2)]
        s_typ = [sem(f"s_typ{j}") for j in range(2)]
        s_toh = sem("s_toh")
        s_cps = sem("s_cps")
        s_msg = sem("s_msg")
        s_relu = sem("s_relu")
        s_oh = [sem(f"s_oh{l}") for l in range(2)]
        s_agg = [sem(f"s_agg{l}") for l in range(2)]
        s_acc = [sem(f"s_acc_l{l}") for l in range(2)]
        s_rcnt = sem("s_rcnt")
        s_noedge = sem("s_noedge")
        s_hst = sem("s_hst")
        s_hnT = sem("s_hnT")
        s_st = [sem(f"s_st{l}") for l in range(2)]
        s_y = [sem(f"s_y{l}") for l in range(2)]
        s_x1 = [sem(f"s_x1_l{l}") for l in range(2)]
        s_var = [sem(f"s_var_l{l}") for l in range(2)]
        s_std = [sem(f"s_std_l{l}") for l in range(2)]
        s_nb = [sem(f"s_nb_l{l}") for l in range(2)]
        s_h1 = sem("s_h1")
        s_keep = sem("s_keep")
        s_hT = sem("s_hT")
        s_hTs = sem("s_hTs")
        s_p = sem("s_p")
        s_ps = sem("s_ps")
        s_acc0 = sem("s_acc0")
        s_z = sem("s_z")
        s_zg = sem("s_zg")
        s_fin = sem("s_fin")
        s_out = sem("s_out")
        s_bn0 = sem("s_bn0")
        s_bn = [sem(f"s_bn_l{l}") for l in range(2)]
        s_step = [sem(f"s_step{l}") for l in range(2)]
        s_dcur = [sem(f"s_dcur{l}") for l in range(2)]
        s_none = sem("s_none")
        s_xb = sem("s_xb")
        s_ones16 = sem("s_ones16")
        s_prep = sem("s_prep")
        s_hhi = sem("s_hhi")
        s_hlo = sem("s_hlo")
        s_cols = sem("s_cols")
        s_zhot = sem("s_zhot")
        s_build = sem("s_build")
        s_evac = sem("s_evac")
        s_dense = sem("s_dense")
        s_sums = sem("s_sums")
        s_place = sem("s_place")
        s_merge = sem("s_merge")
        s_dacc = sem("s_dacc")
        s_apart = sem("s_apart")

        NIN = 22
        block = ctx.enter_context(nc.Block())

        def apart(eng):
            eng.sem_inc(s_apart, 1)

        def pairs(eng, body):
            for j in range(2):
                body(j, j, True)
            with eng.Fori(1, PAIRS) as i:
                for j in range(2):
                    body(i * 2 + j, j, False)

        def blocks(eng, body):
            for b in range(4):
                body(b, b % 2, True, b > 0, b > 1, False)
            with eng.Fori(2, BLOCKS // 2) as i:
                for j in range(2):
                    body(i * 2 + j, j, True, True, True, True)
            body(BLOCKS, 0, False, True, True, True)
            body(BLOCKS + 1, 1, False, False, True, True)

        def chunks(eng, body):
            body(0, True)
            with eng.Fori(1, CHUNKS) as c:
                body(c, False)

        @block.sync
        def _(sp):
            sp.wait_ge(s_pad, 1)
            sp.dma_start(xs[:, 0:TILES - 1, :],
                         x[0:(TILES - 1) * P, :].rearrange("(t p) d -> p t d", p=P)).then_inc(s_x, 16)
            sp.dma_start(xs[0:LASTROWS, TILES - 1, :], x[(TILES - 1) * P:N, :]).then_inc(s_x, 16)
            sp.dma_start(chk_a, dst_flat[0:FR * P].rearrange("(p n) -> p n", p=P)).then_inc(s_chk, 16)
            sp.dma_start(chk_b, dst_flat[1:FR * P + 1].rearrange("(p n) -> p n", p=P)).then_inc(s_chk, 16)
            sp.dma_start(tail_a, dst_flat[None, FR * P:n_edges - 1]).then_inc(s_chk, 16)
            sp.dma_start(tail_b, dst_flat[None, FR * P + 1:n_edges]).then_inc(s_chk, 16)
            sp.dma_start(ends_i[:, 0:1], dst_flat[None, 0:1]).then_inc(s_chk, 16)
            sp.dma_start(ends_i[:, 1:2], dst_flat[None, n_edges - 1:n_edges]).then_inc(s_chk, 16)
            loads = [(kc[:, :], consts), (w0[:, :], w0t), (wx[:, :], wxt), (wu[:, :], updt),
                     (wet_s[:, :], wet), (dst_i[:, :], dst_t), (src_i, src_t),
                     (tfirst_i, tfirst.to_broadcast([P, ALLT])), (tlast_i, tlast), (blast_i, blast), (trep_i, trep),
                     (bfirst_i[:, :], bfirst.to_broadcast([P, BLOCKS + 1])), (gfirst_i[:, :], gfirst.to_broadcast([P, GROUPS])),
                     (glast_i[:, :], glast)]
            loads += [(emb_s[:, k * NT:(k + 1) * NT], embt) for k in range(3)]
            loads += [(r, v.to_broadcast([P, D])) for r, v in
                      zip((b0r, msgbr, updbr, lngr, lnbr), (b0, msgb, updb, lng, lnb))]
            assert len(loads) == NIN
            for to, of in loads:
                sp.dma_start(to, of).then_inc(s_in, 16)

            sp.wait_ge(s_h0, TILES)
            sp.dma_start(table0.rearrange("(t p) d -> p t d", p=P), hs[:, :, :]).then_inc(s_tab[0], 16)

            def load_edges(l, n, j, first):
                if not first:
                    sp.wait_ge(s_gath[l][j], (n - j) * (8 * TPG))
                sp.dma_start(idxb[:, j, :], idx_g[n]).then_inc(s_idx[l][j], 16)
                if l:
                    if not first:
                        sp.wait_ge(s_toh, n - 1)
                    sp.dma_start(types[:, j, :], types_g[n].to_broadcast([K3, TPG * P])).then_inc(s_typ[j], 16)

            sp.wait_ge(s_flag, 1)
            flag_sp = sp.value_load(flag[0:1, 0:1], min_val=0, max_val=1)
            with sp.If(flag_sp != 0):
                pairs(sp, lambda n, j, first: load_edges(0, n, j, first))
            t1 = table1.rearrange("(c j p) d -> c p j d", j=RING, p=P)
            with sp.Fori(0, CHUNKS) as c:
                sp.wait_ge(s_ps, (c + 1) * RING)
                sp.dma_start(t1[c], st_o[:, :, :]).then_inc(s_tab[1], 16)
            pairs(sp, lambda n, j, first: load_edges(1, n, j, first))

            oc = out[0:(CHUNKS - 1) * RING * P, :].rearrange("(c j p) d -> c p j d", j=RING, p=P)
            with sp.Fori(0, CHUNKS - 1) as c:
                sp.wait_ge(s_fin, (c + 1) * RING)
                sp.dma_start(oc[c], st_o[:, :, :]).then_inc(s_out, 16)
            sp.wait_ge(s_fin, TILES)
            at = (CHUNKS - 1) * RING * P
            sp.dma_start(out[at:at + (RING - 1) * P, :].rearrange("(j p) d -> p j d", p=P),
                         st_o[:, 0:RING - 1, :]).then_inc(s_out, 16)
            sp.dma_start(out[(TILES - 1) * P:N, :], st_o[0:LASTROWS, RING - 1, :]).then_inc(s_out, 16)
            sp.wait_ge(s_out, (CHUNKS + 1) * 16)

        @block.gpsimd
        def _(pool):
            nc.gpsimd.memset(xs[:, TILES - 1, :], 0.0).then_inc(s_pad, 1)
            nc.gpsimd.memset(accT[:, :], 0.0).then_inc(s_acc[0], 1)
            nc.gpsimd.memset(cntT[:, :], 0.0).then_inc(s_zero, 1)
            pool.wait_ge(s_zero, 1)
            pool.wait_ge(s_acc[0], 1)
            pool.sem_inc(s_dacc, 1)
            nc.gpsimd.memset(ones[:, :], 1.0).then_inc(s_zero, 1)
            nc.gpsimd.memset(h_hi[:, :, D:D + 1], SCALE).then_inc(s_ones16, 1)
            pool.wait_ge(s_viol, 1)
            nc.gpsimd.partition_all_reduce(vmax[:, 1:2], vmax[:, 0:1], P, RMAX).then_inc(s_vmax, 1)

            def gather(l, n, j, first):
                table = (table0, table1)[l]
                pool.wait_ge(s_idx[l][j], (n - j) * 8 + 16)
                if not first:
                    if l:
                        pool.wait_ge(s_msg, (n - 1) * len(CH))
                    else:
                        pool.wait_ge(s_gfree[0], n - 1)
                apart(pool)
                for k in range(TPG):
                    pool.indirect_dma_start(
                        gath[:, j, k, :], None, table,
                        bass.IndirectOffsetOnAxis(ap=idxb[:, j, k:k + 1].bitcast(U32), axis=0),
                    ).then_inc(s_gath[l][j], 16)

            pool.wait_ge(s_in, 16 * NIN)
            pool.wait_ge(s_h0, TILES)
            nc.gpsimd.tensor_tensor(xs[:, :, :], xs[:, :, :], rows[:, 0:1, :].to_broadcast([P, TILES, D]),
                                    ALU.add).then_inc(s_xb, 1)
            pool.wait_ge(s_tab[0], 16)
            pool.wait_ge(s_flag, 1)
            flag_pool = pool.value_load(flag[0:1, 0:1], min_val=0, max_val=1)
            with pool.If(flag_pool != 0):
                pool.wait_ge(s_prep, 1)
                pairs(pool, lambda n, j, first: gather(0, n, j, first))

            with pool.Fori(0, CHUNKS) as c:
                for j in range(RING):
                    pool.wait_ge(s_h1, c * RING + (j + 1))
                    nc.gpsimd.tensor_tensor(hs[:, bass.ds(c * RING + j, 1), :], st_h[:, j:j + 1, :],
                                            rows[:, 2:3, :], ALU.add).then_inc(s_keep, 1)
                    nc.gpsimd.tensor_tensor(xs[:, bass.ds(c * RING + j, 1), :], xs[:, bass.ds(c * RING + j, 1), :],
                                            rows[:, 4:5, :], ALU.add).then_inc(s_keep, 1)
            pool.wait_ge(s_tab[1], 16 * CHUNKS)
            pairs(pool, lambda n, j, first: gather(1, n, j, first))

            def finish_rows(c, first):
                for j in range(RING):
                    pool.wait_ge(s_z, c * RING + (j + 1))
                    nc.gpsimd.tensor_tensor(st_t[:, j:j + 1, :], st_h[:, j:j + 1, :],
                                            rows[:, 3:4, :], ALU.mult).then_inc(s_zg, 1)
                    if j == 0:
                        if not first:
                            pool.wait_ge(s_out, c * 16)
                    pool.wait_ge(s_zg, c * RING + (j + 1))
                    nc.gpsimd.tensor_tensor(st_o[:, j:j + 1, :], st_t[:, j:j + 1, :],
                                            xs[:, bass.ds(c * RING + j, 1), :], ALU.add).then_inc(s_fin, 1)

            chunks(pool, finish_rows)

        @block.scalar
        def _(act):
            act.wait_ge(s_var0, 1)
            nc.scalar.activation(small[:, 5, :], small[:, 4, :], ACT.Sqrt, bias=epsc[:, 0:1],
                                 scale=1.0 / D).then_inc(s_std0, 1)
            act.wait_ge(s_nb0, 1)
            with act.Fori(0, CHUNKS) as c:
                for j in range(RING):
                    t = c * RING + j
                    nc.scalar.activation(hs[:, t, :], xs[:, t, :], ACT.Relu, bias=nb0[:, bass.ds(t, 1)],
                                         scale=rstd0[:, bass.ds(t, 1)]).then_inc(s_h0, 1)
                act.wait_ge(s_h0, c * RING + RING)
                some = bass.ds(c * RING, RING)
                nc.scalar.activation(h_hi[:, some, 0:D], hs[:, some, :], ACT.Copy, scale=SCALE).then_inc(s_hhi, 1)
            act.wait_ge(s_flag, 1)
            flag_act = act.value_load(flag[0:1, 0:1], min_val=0, max_val=1)

            def copy_out(b, j, build, dense, merge, steady):
                if build:
                    if merge:
                        act.wait_ge(s_dense, b - 1)
                    for t in range(TPB):
                        act.wait_ge(s_build, b * TPB + (t + 1))
                        nc.scalar.activation(adj[:, j, :, t * WT:(t + 1) * WT],
                                             ps[:, (j * TPB + t) % 4, 0:ZC].rearrange("p (h w) -> p h w", w=WT),
                                             ACT.Copy).then_inc(s_evac, 1)
                if dense:
                    act.wait_ge(s_dense, b)
                    if merge:
                        act.wait_ge(s_merge, b - 1)
                    nc.scalar.activation(sums[:, :], ps[0:ROWS, 5 - j, 0:D + 1], ACT.Copy,
                                         scale=1.0 / SCALE).then_inc(s_sums, 1)

            with act.If(flag_act == 0):
                blocks(act, copy_out)

            def table_rows(c, first):
                act.wait_ge(s_var[0], c + 1)
                nc.scalar.activation(csmall[:, 5, :], csmall[:, 4, :], ACT.Sqrt, bias=epsc[:, 0:1],
                                     scale=1.0 / D).then_inc(s_std[0], 1)
                act.wait_ge(s_nb[0], c + 1)
                if not first:
                    act.wait_ge(s_keep, c * (2 * RING))
                if not first:
                    act.wait_ge(s_hT, c * RING)
                for j in range(RING):
                    nc.scalar.activation(st_h[:, j, :], xs[:, c * RING + j, :], ACT.Relu, bias=nb1[:, j:j + 1],
                                         scale=rstd1[:, j:j + 1]).then_inc(s_h1, 1)
                for j in range(RING):
                    act.wait_ge(s_hT, c * RING + bank_full(j))
                    nc.scalar.activation(st_t[:, j, :], slot(2, j), ACT.Copy).then_inc(s_hTs, 1)
                if not first:
                    act.wait_ge(s_tab[1], c * 16)
                for j in range(RING):
                    act.wait_ge(s_p, c * RING + bank_full(j))
                    nc.scalar.activation(st_o[:, j, :], slot(4, j), ACT.Copy).then_inc(s_ps, 1)

            chunks(act, table_rows)

            def relu_messages(n, j, first):
                for c, w in enumerate(CH):
                    act.wait_ge(s_msg, n * len(CH) + (c + 1))
                    m = msg[:, SLOT0[c]:SLOT0[c] + w, :]
                    nc.scalar.activation(m, m, ACT.Relu).then_inc(s_relu, 1)

            pairs(act, relu_messages)

            def normalise(c, first):
                act.wait_ge(s_var[1], c + 1)
                nc.scalar.activation(csmall[:, 5, :], csmall[:, 4, :], ACT.Sqrt, bias=epsc[:, 0:1],
                                     scale=1.0 / D).then_inc(s_std[1], 1)
                act.wait_ge(s_nb[1], c + 1)
                if not first:
                    act.wait_ge(s_zg, c * RING)
                for j in range(RING):
                    nc.scalar.activation(st_h[:, j, :], hs[:, c * RING + j, :], ACT.Identity, bias=nb1[:, j:j + 1],
                                         scale=rstd1[:, j:j + 1]).then_inc(s_z, 1)

            chunks(act, normalise)

        @block.tensor
        def _(pe):
            pe.wait_ge(s_in, 16 * NIN)
            nc.tensor.matmul(slot(0, 0)[0:K3, :], emb_s[:, :], wet_s[:, :], start=True, stop=True).then_inc(s_cps0, 1)
            pe.wait_ge(s_zero, 2)
            pe.wait_ge(s_flag, 1)
            flag_pe = pe.value_load(flag[0:1, 0:1], min_val=0, max_val=1)

            def type_terms(n, first):
                pe.wait_ge(s_toh, n + 1)
                if not first:
                    pe.wait_ge(s_msg, n * len(CH))
                for c, w in enumerate(CH):
                    for k in range(w):
                        last = nc.tensor.matmul(ps[:, c, k * P:(k + 1) * P], typehot[:, SLOT0[c] + k, :],
                                                csel[:, :], start=True, stop=True)
                    last.then_inc(s_cps, 1)

            def window_sums(l, n, j, q):
                rows_of = (gath[:, j], msg)[l]
                pe.wait_ge(s_oh[l], q + 1)
                for k in range(TPG):
                    if l and k in SLOT0:
                        pe.wait_ge(s_relu, n * len(CH) + (SLOT0.index(k) + 1))
                    last = nc.tensor.matmul(psA, rows_of[:, k, :], onehot[:, k, :], start=(k == 0), stop=(k == TPG - 1))
                if l == 0:
                    for k in range(TPG):
                        last = nc.tensor.matmul(psN, ones[:, :], onehot[:, k, :], start=(k == 0), stop=(k == TPG - 1))
                last.then_inc(s_agg[l], 1)

            def dense_block(b, j, build, dense, merge, steady):
                if dense:
                    pe.wait_ge(s_evac, b * TPB)
                    if steady or b == 3:
                        pe.wait_ge(s_sums, b - 2)
                acc = ps[0:ROWS, 5 - j, :]
                for t in range(TPB):
                    if build:
                        pe.wait_ge(s_zhot, b * TPB + (t + 1))
                        if dense or t >= 4:
                            pe.wait_ge(s_evac, b * TPB + (t - 3))
                        nc.tensor.matmul(ps[:, (j * TPB + t) % 4, 0:ZC], lohot[:, t, :], zhot[:, t, 0:ZC],
                                         start=True, stop=True).then_inc(s_build, 1)
                    if dense:
                        for h in range(t * TILES // TPB, (t + 1) * TILES // TPB):
                            a = adj[:, 1 - j, h, :]
                            nc.tensor.matmul(acc[:, 0:D + 1], a, h_hi[:, h, :], start=(h == 0), stop=False)
                            last = nc.tensor.matmul(acc[:, 0:D], a, h_lo[:, h, :], start=False, stop=(h == TILES - 1))
                if dense:
                    last.then_inc(s_dense, 1)
                if merge:
                    pe.wait_ge(s_sums, b - 1)
                    pe.wait_ge(s_place, b - 1)
                    if steady:
                        pe.wait_ge(s_dacc, b * 2 - 5)
                    nc.tensor.matmul(ps[:, 6 + j, 0:WB], sums[:, 0:D], place[:, j, :], start=True, stop=True)
                    nc.tensor.matmul(ps[:, 6 + j, WB:2 * WB], sums[:, D:D + 1].to_broadcast([ROWS, P]),
                                     place[:, j, :], start=True, stop=True).then_inc(s_merge, 1)

            def layer(l):
                def group(n, j, first, windows):
                    if l:
                        type_terms(n, first and j == 0)
                    else:
                        pe.wait_ge(s_gath[0][j], (n - j) * (8 * TPG) + 16 * TPG)
                    if windows:
                        apart(pe)
                        with pe.Fori(0, NW) as w:
                            window_sums(l, n, j, n * NW + w)
                    else:
                        window_sums(l, n, j, n)

                def no_edges(t):
                    pe.wait_ge(s_hst, t + 1)
                    nc.tensor.transpose(slot(0, 0), st_h[:, 0, :], ident).then_inc(s_hnT, 1)

                with pe.If(flag_pe == 0):
                    if l:
                        pairs(pe, lambda n, j, first: group(n, j, first, False))
                    else:
                        pe.wait_ge(s_hhi, CHUNKS)
                        pe.wait_ge(s_hlo, CHUNKS)
                        pe.wait_ge(s_ones16, 1)
                        blocks(pe, dense_block)
                with pe.Else():
                    pairs(pe, lambda n, j, first: group(n, j, first, True))
                    if l == 0:
                        with pe.Fori(0, TILES) as t:
                            no_edges(t)

            layer(0)
            def node_products(c, first):
                if not first:
                    pe.wait_ge(s_x1[0], c * RING)
                for j in range(RING):
                    pe.wait_ge(s_st[0], c * RING + (j + 1))
                    nc.tensor.matmul(slot(0, j), st_a[:, j, :], w0[:, :], start=True, stop=True).then_inc(s_y[0], 1)
                if not first:
                    pe.wait_ge(s_hTs, c * RING)
                for j in range(RING):
                    pe.wait_ge(s_h1, c * RING + (j + 1))
                    nc.tensor.transpose(slot(2, j), st_h[:, j, :], ident).then_inc(s_hT, 1)
                if not first:
                    pe.wait_ge(s_ps, c * RING)
                for j in range(RING):
                    pe.wait_ge(s_hTs, c * RING + (j + 1))
                    nc.tensor.matmul(slot(4, j), st_t[:, j, :], wx[:, :], start=True, stop=True).then_inc(s_p, 1)

            chunks(pe, node_products)
            layer(1)
            def update_products(c, first):
                if not first:
                    pe.wait_ge(s_x1[1], c * RING)
                for j in range(RING):
                    pe.wait_ge(s_st[1], c * RING + (j + 1))
                    nc.tensor.matmul(slot(0, j), st_a[:, j, :], wu[:, :], start=True, stop=True).then_inc(s_y[1], 1)

            chunks(pe, update_products)

        @block.vector
        def _(dve):
            chained = [0]

            def chain(ins):
                chained[0] += 1
                ins.then_inc(s_dve, 1)
                dve.wait_ge(s_dve, chained[0])

            def spread(st, sm, step):
                me, qe, mo, qo = (st[:, :, k] for k in (1, 2, 4, 5))
                step(nc.vector.tensor_tensor(sm[:, 0, :], me, mo, ALU.add))
                step(nc.vector.tensor_tensor(sm[:, 1, :], me, mo, ALU.subtract))
                step(nc.vector.tensor_tensor(sm[:, 2, :], qe, qo, ALU.add))
                step(nc.vector.tensor_tensor(sm[:, 3, :], sm[:, 1, :], sm[:, 1, :], ALU.mult))
                return nc.vector.scalar_tensor_tensor(sm[:, 4, :], sm[:, 3, :], D / 4.0, sm[:, 2, :],
                                                      ALU.mult, ALU.add)

            nc.vector.memset(epsc[:, :], EPS)
            chain(nc.vector.memset(viol[:, :], 0.0))
            dve.wait_ge(s_x, 32)
            with dve.Fori(0, CHUNKS) as c:
                for j in range(RING):
                    nc.vector.bn_stats(stats[:, c * RING + j, :], xs[:, c * RING + j, :]).then_inc(s_bn0, 1)
            dve.wait_ge(s_bn0, TILES)
            spread(stats, small, chain).then_inc(s_var0, 1)
            dve.wait_ge(s_std0, 1)
            chain(nc.vector.reciprocal(rstd0[:, :], small[:, 5, :]))
            nc.vector.scalar_tensor_tensor(nb0[:, :], small[:, 0, :], -0.5, rstd0[:, :],
                                           ALU.mult, ALU.mult).then_inc(s_nb0, 1)

            dve.wait_ge(s_chk, 16 * 6)
            dve.wait_ge(s_in, 16 * NIN)
            chain(nc.vector.tensor_tensor(chk_d, chk_b, chk_a, ALU.subtract))
            chain(nc.vector.tensor_tensor(tail_d, tail_b, tail_a, ALU.subtract))
            chain(nc.vector.tensor_reduce(dmm[:, 0:1], chk_d, AX.X, ALU.max))
            chain(nc.vector.tensor_reduce(dmm[:, 1:2], chk_d, AX.X, ALU.min))
            chain(nc.vector.tensor_reduce(dmm[0:1, 2:3], tail_d, AX.X, ALU.max))
            chain(nc.vector.tensor_reduce(dmm[0:1, 3:4], tail_d, AX.X, ALU.min))
            chain(nc.vector.tensor_scalar(viol[:, 0:1], dmm[:, 0:1], -1.0, None, ALU.add))
            chain(nc.vector.tensor_scalar(viol[:, 1:2], dmm[:, 1:2], -1.0, None, ALU.mult))
            chain(nc.vector.tensor_scalar(viol[0:1, 2:3], dmm[0:1, 2:3], -1.0, None, ALU.add))
            chain(nc.vector.tensor_scalar(viol[0:1, 3:4], dmm[0:1, 3:4], -1.0, None, ALU.mult))
            chain(nc.vector.tensor_copy(viol[0:1, 4:5], ends_i[0:1, 0:1]))
            chain(nc.vector.tensor_scalar(viol[0:1, 5:6], ends_i[0:1, 1:2], -1.0, float(N - 1), ALU.mult, ALU.add))
            for k, (late, early, width) in enumerate(((glast_i[0:1, :], gfirst_i[0:1, :], W),
                                                      (blast_i, bfirst_i[0:1, :], WB), (tlast_i, tfirst_i[0:1, :], WT))):
                span = spans[0:1, 0:late.shape[1]]
                v = viol[0:1, 6 + k:7 + k]
                chain(nc.vector.tensor_tensor(span, late, early, ALU.subtract))
                chain(nc.vector.tensor_reduce(v, span, AX.X, ALU.max))
                chain(nc.vector.tensor_scalar(v, v, -float(width - 1), None, ALU.add))
            nc.vector.tensor_reduce(vmax[:, 0:1], viol[:, :], AX.X, ALU.max).then_inc(s_viol, 1)
            dve.wait_ge(s_vmax, 1)
            nc.vector.tensor_scalar(flag[:, :], vmax[:, 1:2], 0.0, None, ALU.is_gt).then_inc(s_flag, 1)
            one_window = dmm[:, 0:1]
            chain(nc.vector.tensor_scalar(one_window, vmax[:, 1:2], 0.0, None, ALU.is_le))
            base = spans[:, 0:GROUPS]
            chain(nc.vector.tensor_scalar(base, gfirst_i[:, :], one_window, None, ALU.mult))
            chain(nc.vector.tensor_tensor(dst_r[:, :, :],
                                          dst_i[:, 0:GROUPS * TPG].rearrange("p (g t) -> p g t", t=TPG),
                                          base[:, :, None].to_broadcast([P, GROUPS, TPG]), ALU.subtract))

            src_hi = chk_a_all
            chain(nc.vector.tensor_scalar(src_hi, src_i, 7, None, ALU.logical_shift_right))
            chain(nc.vector.tensor_scalar(src_i, src_i, P - 1, None, ALU.bitwise_and))
            chain(nc.vector.tensor_copy(src_lo[:, :], src_i))
            chain(nc.vector.tensor_tensor(code, dst_i[:, :], tfirst_i, ALU.subtract))
            chain(nc.vector.scalar_tensor_tensor(code, src_hi, float(WT), code, ALU.mult, ALU.add))
            chain(nc.vector.tensor_tensor(vrow[:, :], trep_i, bfirst_i[0:ROWS, :], ALU.subtract))
            chain(nc.vector.tensor_scalar(vrow[:, :], vrow[:, :], kc[0:ROWS, KI + 4:KI + 5], None, ALU.add))
            nc.vector.tensor_copy(iota16[:, :], kc[:, P:P + ZP]).then_inc(s_prep, 1)
            dve.wait_ge(s_prep, 1)

            dve.wait_ge(s_cps0, 1)
            chain(nc.vector.tensor_tensor(cmat[:, 0, :], slot(0, 0)[0:K3, :], msgbr[0:K3, :], ALU.add))
            chain(nc.vector.tensor_copy(cpart[:, 0, :], cmat[:, 0, :]))
            chain(nc.vector.tensor_tensor(cmat[:, 1, :], cmat[:, 0, :], cpart[:, 0, :], ALU.subtract))
            chain(nc.vector.tensor_copy(cpart[:, 1, :], cmat[:, 1, :]))
            chain(nc.vector.tensor_tensor(cmat[:, 2, :], cmat[:, 1, :], cpart[:, 1, :], ALU.subtract))
            chain(nc.vector.tensor_copy(cpart[:, 2, :], cmat[:, 2, :]))
            third = [kc[0:K3, KI + 1 + k:KI + 2 + k] for k in range(3)]
            chain(nc.vector.tensor_scalar(cmat[:, 0, :], cpart[:, 0, :], third[0], None, ALU.mult))
            chain(nc.vector.scalar_tensor_tensor(cmat[:, 1, :], cpart[:, 1, :], third[1], cmat[:, 0, :],
                                                 ALU.mult, ALU.add))
            nc.vector.scalar_tensor_tensor(csel[:, :], cpart[:, 2, :], third[2], cmat[:, 1, :],
                                           ALU.mult, ALU.add).then_inc(s_csel, 1)

            with dve.Fori(0, CHUNKS) as c:
                some = bass.ds(c * RING, RING)
                dve.wait_ge(s_hhi, c + 1)
                nc.vector.scalar_tensor_tensor(h_lo[:, some, :], hs[:, some, :], SCALE, h_hi[:, some, 0:D],
                                               ALU.mult, ALU.subtract).then_inc(s_hlo, 1)
            dve.wait_ge(s_hlo, CHUNKS)
            dve.wait_ge(s_zero, 2)
            flag_dve = dve.value_load(flag[0:1, 0:1], min_val=0, max_val=1)

            def columns_of(b, j):
                at = bass.ds(b * TPB, TPB)
                nc.vector.tensor_copy(cols[:, j, 0, :], code[:, at]).then_inc(s_cols, 1)
                nc.vector.tensor_copy(cols[:, j, 1, :], src_lo[:, at]).then_inc(s_cols, 1)

            def one_hots(b, j, dense):
                dve.wait_ge(s_cols, b * 2 + 2)
                for t in range(TPB):
                    if dense:
                        dve.wait_ge(s_build, b * TPB + (t + 1 - TPB))
                    nc.vector.tensor_scalar(zhot[:, t, :], iota16[:, :], cols[:, j, 0, t:t + 1], None, ALU.is_equal)
                    nc.vector.tensor_scalar(lohot[:, t, :], iota16[:, 0:P], cols[:, j, 1, t:t + 1], None,
                                            ALU.is_equal).then_inc(s_zhot, 1)
                    if t == TPB // 2:
                        if dense:
                            dve.wait_ge(s_zhot, b * TPB)
                        columns_of(b + 1, 1 - j)

            def load_places(b):
                return nc.values_load_multi_w_load_instructions(
                    bfirst_i[0:1, bass.ds(b, 2)], engines=[dve.engine], min_val=0, max_val=N - 1)[1]

            def place_block(b, j):
                nc.vector.tensor_scalar(place[:, j, :], kc[0:ROWS, P:P + WB], vrow[:, bass.ds(b, 1)], None,
                                        ALU.is_equal).then_inc(s_place, 1)

            def add_block(b, j, col):
                dve.wait_ge(s_merge, b + 1)
                dve.wait_ge(s_dacc, b * 2 + 1)
                for k, total in enumerate((accT, cntT)):
                    nc.vector.tensor_tensor(total[:, bass.ds(col, WB)], total[:, bass.ds(col, WB)],
                                            ps[:, 6 + j, k * WB:(k + 1) * WB], ALU.add).then_inc(s_dacc, 1)

            def dense_blocks():
                columns_of(0, 0)
                one_hots(0, 0, False)
                one_hots(1, 1, True)
                place_block(0, 0)
                one_hots(2, 0, True)
                place_block(1, 1)
                col = load_places(0)
                one_hots(3, 1, True)
                add_block(0, 0, col[0])
                place_block(2, 0)
                with dve.Fori(2, BLOCKS // 2) as i:
                    col = load_places(i * 2 - 3)
                    for j in range(2):
                        one_hots(i * 2 + j, j, True)
                        add_block(i * 2 + (j - 3), 1 - j, col[j])
                        place_block(i * 2 + (j - 1), 1 - j)
                col = load_places(BLOCKS - 3)
                add_block(BLOCKS - 3, 1, col[0])
                place_block(BLOCKS - 1, 1)
                add_block(BLOCKS - 2, 0, col[1])
                col = load_places(BLOCKS - 2)
                add_block(BLOCKS - 1, 1, col[1])
                dve.wait_ge(s_dacc, 2 * BLOCKS + 1)

            def make_onehot(l, q, dst):
                dve.wait_ge(s_acc[l], q * (2 - l) + 1)
                nc.vector.tensor_tensor(onehot[:, :, :], kc[:, None, P:P + W].to_broadcast([P, TPG, W]),
                                        dst[:, :, None].to_broadcast([P, TPG, W]), ALU.is_equal).then_inc(s_oh[l], 1)

            def add_window(l, q, col):
                dve.wait_ge(s_agg[l], q + 1)
                nc.vector.tensor_tensor(accT[:, bass.ds(col, W)], accT[:, bass.ds(col, W)], psA,
                                        ALU.add).then_inc(s_acc[l], 1)
                if l == 0:
                    nc.vector.tensor_tensor(cntT[:, bass.ds(col, W)], cntT[:, bass.ds(col, W)], psN,
                                            ALU.add).then_inc(s_acc[l], 1)

            def messages(n, j):
                dve.wait_ge(s_typ[j], (n - j) * 8 + 16)
                nc.vector.tensor_scalar(typehot[:, :, :].rearrange("k t e -> k (t e)"), types[:, j, :],
                                        kc[0:K3, KI:KI + 1], None, ALU.is_equal).then_inc(s_toh, 1)
                dve.wait_ge(s_gath[1][j], (n - j) * (8 * TPG) + 16 * TPG)
                for c, w in enumerate(CH):
                    dve.wait_ge(s_cps, n * len(CH) + (c + 1))
                    nc.vector.tensor_tensor(msg[:, SLOT0[c]:SLOT0[c] + w, :], gath[:, j, SLOT0[c]:SLOT0[c] + w, :],
                                            ps[:, c, 0:w * P].rearrange("p (t d) -> p t d", d=D),
                                            ALU.add).then_inc(s_msg, 1)

            def layer(l):
                def group(n, j, first):
                    make_onehot(l, n, dst_r[:, n, :])
                    if l:
                        messages(n, j)
                    col = dve.value_load(gfirst_i[0:1, bass.ds(n, 1)], min_val=0, max_val=N - 1)
                    add_window(l, n, col)

                def group_all_windows(n, j, first):
                    if l:
                        messages(n, j)
                    if j or not first:
                        dve.wait_ge(s_dcur[l], n * (NW + 1))
                    nc.vector.tensor_copy(dcur[:, :], dst_r[:, n, :]).then_inc(s_dcur[l], 1)
                    with dve.Fori(0, NW) as w:
                        q = n * NW + w
                        dve.wait_ge(s_dcur[l], n * (NW + 1) + w + 1)
                        make_onehot(l, q, dcur)
                        dve.wait_ge(s_oh[l], q + 1)
                        nc.vector.tensor_scalar(dcur[:, :], dcur[:, :], -float(W), None, ALU.add).then_inc(s_dcur[l], 1)
                        add_window(l, q, w * W)
                    if l == 0:
                        dve.sem_inc(s_gfree[0], 1)

                def no_edges(t):
                    col = bass.ds(t * P, P)
                    nc.vector.tensor_copy(st_h[:, 0, :], hs[:, t, :]).then_inc(s_hst, 1)
                    nc.vector.tensor_scalar(st_a[:, 0, :], cntT[:, col], 0.0, None, ALU.is_equal).then_inc(s_none, 1)
                    dve.wait_ge(s_hnT, t + 1)
                    dve.wait_ge(s_none, t * 3 + 1)
                    nc.vector.tensor_tensor(st_t[:, 0, :], st_a[:, 0, :], slot(0, 0), ALU.mult).then_inc(s_none, 1)
                    dve.wait_ge(s_none, t * 3 + 2)
                    nc.vector.tensor_tensor(accT[:, col], accT[:, col], st_t[:, 0, :], ALU.add).then_inc(s_none, 1)
                    dve.wait_ge(s_none, t * 3 + 3)

                with dve.If(flag_dve == 0):
                    if l:
                        pairs(dve, group)
                        dve.wait_ge(s_acc[1], GROUPS + 1)
                    else:
                        dense_blocks()
                with dve.Else():
                    pairs(dve, group_all_windows)
                    dve.wait_ge(s_acc[l], GROUPS * NW * (2 - l) + 1)
                    if l == 0:
                        with dve.Fori(0, TILES) as t:
                            no_edges(t)

            def nodes(l, c, first):
                steps = [0]

                def step(ins):
                    steps[0] += 1
                    ins.then_inc(s_step[l], 1)
                    dve.wait_ge(s_step[l], c * 5 + steps[0])

                for j in range(RING):
                    col = bass.ds((c * RING + j) * P, P)
                    nc.vector.tensor_tensor(st_a[:, j, :], accT[:, col], cntT[:, col], ALU.mult).then_inc(s_st[l], 1)
                keep = (xs, hs)[l]
                for j in range(RING):
                    t = c * RING + j
                    dve.wait_ge(s_y[l], c * RING + bank_full(j))
                    nc.vector.tensor_tensor(keep[:, t, :], slot(0, j), keep[:, t, :], ALU.add).then_inc(s_x1[l], 1)
                dve.wait_ge(s_x1[l], c * RING + RING)
                apart(dve)
                for j in range(RING):
                    nc.vector.bn_stats(cstats[:, j, :], keep[:, c * RING + j, :]).then_inc(s_bn[l], 1)
                dve.wait_ge(s_bn[l], c * RING + RING)
                spread(cstats, csmall, step).then_inc(s_var[l], 1)
                dve.wait_ge(s_std[l], c + 1)
                if not first:
                    dve.wait_ge((s_h1, s_z)[l], c * RING)
                step(nc.vector.reciprocal(rstd1[:, :], csmall[:, 5, :]))
                nc.vector.scalar_tensor_tensor(nb1[:, :], csmall[:, 0, :], -0.5, rstd1[:, :],
                                               ALU.mult, ALU.mult).then_inc(s_nb[l], 1)

            layer(0)
            dve.wait_ge(s_xb, 1)
            chain(nc.vector.tensor_scalar(cntT[:, :], cntT[:, :], 1.0, None, ALU.max))
            chain(nc.vector.reciprocal(cntT[:, :], cntT[:, :]))
            chunks(dve, lambda c, first: nodes(0, c, first))
            dve.wait_ge(s_st[0], TILES)
            nc.vector.memset(accT[:, :], 0.0).then_inc(s_acc[1], 1)
            layer(1)
            dve.wait_ge(s_keep, 2 * TILES)
            chunks(dve, lambda c, first: nodes(1, c, first))


def kernel(x, src, dst, edge_type_16, L0_gnn_W, L0_gnn_b, L1_gnn_edge_emb_W, L1_gnn_msg_W, L1_gnn_msg_b,
           L1_gnn_upd_W, L1_gnn_upd_b, L1_gnn_ln_g, L1_gnn_ln_b):
    import numpy as np
    import concourse.bacc as bacc
    from concourse.bass_utils import run_bass_kernel_spmd

    x, src, dst, typ = (np.asarray(a) for a in (x, src, dst, edge_type_16))
    N, D = x.shape
    E = src.shape[0]
    per = TPG * P
    groups = -(-E // per)
    groups += groups % 2
    tiles = -(-groups * TPG // TPB) * TPB
    tiles += tiles % (2 * TPB) + TPB

    def padded(a, value, n):
        return np.concatenate([a, np.full((n - E,), value, a.dtype)])

    def ends(size):
        first = np.minimum(np.arange(0, tiles * P, size), E - 1)
        return first, np.minimum(first + size, E) - 1

    src_p, typ_p = (padded(a, 0, groups * per) for a in (src, typ))
    src_q, dst_q = padded(src, 0, tiles * P), padded(dst, 1 << 20, tiles * P)
    gfirst, glast = (e[:groups] for e in ends(per))
    bfirst, blast = ends(TPB * P)
    tlast = ends(P)[1]
    tfirst = dst_q[::P]
    niota = max(P, WB, -(-N // P) * WT + 3)
    consts = np.zeros((P, P + niota + 5), np.float32)
    consts[:, 0:P] = np.eye(P)
    consts[:, P:P + niota] = np.arange(niota)
    consts[:, P + niota] = np.arange(P) % 16
    for k in range(3):
        consts[16 * k:16 * k + 16, P + niota + 1 + k] = 1.0
    consts[:, P + niota + 4] = np.arange(P) % WT
    row = lambda a: np.asarray(a).reshape(1, -1)
    cols = lambda a: np.ascontiguousarray(np.asarray(a).T)
    msg_w = np.asarray(L1_gnn_msg_W)
    arrays = {
        "x": x,
        "idx_g": np.ascontiguousarray(src_p.reshape(groups, TPG, P).transpose(0, 2, 1)),
        "src_t": np.ascontiguousarray(src_q.reshape(tiles, P).T),
        "dst_t": np.ascontiguousarray(dst_q.reshape(tiles, P).T),
        "dst_flat": dst,
        "tfirst": row(tfirst),
        "tlast": row(dst[tlast]),
        "bfirst": row(dst[bfirst]),
        "blast": row(dst[blast]),
        "trep": np.ascontiguousarray(np.repeat(tfirst.reshape(-1, TPB), WT, axis=1).T),
        "gfirst": row(dst[gfirst]),
        "glast": row(dst[glast]),
        "types_g": typ_p.reshape(groups, 1, per),
        "w0t": cols(L0_gnn_W),
        "b0": row(L0_gnn_b),
        "embt": cols(L1_gnn_edge_emb_W),
        "wet": cols(msg_w[:, D:]),
        "wxt": cols(msg_w[:, :D]),
        "msgb": row(L1_gnn_msg_b),
        "updt": cols(L1_gnn_upd_W),
        "updb": row(L1_gnn_upd_b),
        "lng": row(L1_gnn_ln_g),
        "lnb": row(L1_gnn_ln_b),
        "consts": consts,
    }
    nc = bacc.Bacc("TRN2", target_bir_lowering=False, num_devices=1)
    args = [nc.dram_tensor(k, a.shape, mybir.dt.from_np(a.dtype), kind="ExternalInput").ap()
            for k, a in arrays.items()]
    out = nc.dram_tensor("out", (N, D), F32, kind="ExternalOutput").ap()
    gnn_program(nc, *args, out, E)
    r = run_bass_kernel_spmd(nc, [arrays], core_ids=[0])
    return r.results[0]["out"]
```

```python
from contextlib import ExitStack

import concourse.bass as bass
from concourse import mybir

P = 128
W = 64
TPG = 14
GATHERED = TPG - 1
CH = (4, 4, 3, 2, 1)
BANK = (0, 1, 2, 3, 3)
RUN = 13
TPG0 = 17
W0 = 80
TPR = 3
WT = 7
TPB = 18
WB = 96
SCALE = 4096.0
RING = 7
EPS = 1e-5

F32 = mybir.dt.float32
BF16 = mybir.dt.bfloat16
F16 = mybir.dt.float16
I32 = mybir.dt.int32
U32 = mybir.dt.uint32
ALU = mybir.AluOpType
ACT = mybir.ActivationFunctionType
AX = mybir.AxisListType
RMAX = bass.bass_isa.ReduceOp.max


def gnn_program(nc, x, idx_g, idx0_g, pick_g, src_t, dst_t, dst_flat, tfirst, tfirst_p, tlast_p,
                bfirst, blast, trep, gfirst, glast,
                gfirst0, glast0, types_g, w0t, b0, embt, wet, wxt, msgb,
                updt, updb, lng, lnb, consts, out, n_edges):
    N, D = x.shape
    TILES = -(-N // P)
    CHUNKS = TILES // RING
    GROUPS = idx_g.shape[0]
    PAIRS = GROUPS // 2
    NW = TILES * P // W
    STRIDE = (GROUPS - 4) // (2 * (CHUNKS - 1)) * 2
    NCOL = TILES * P + WB
    LASTROWS = N - (TILES - 1) * P
    SLOT0 = [sum(CH[:c]) for c in range(len(CH))]
    NT = 16
    K3 = 3 * NT
    FR = (n_edges - 1) // P
    TAIL = n_edges - 1 - FR * P
    ALLT = src_t.shape[1]
    GROUPS0 = idx0_g.shape[0]
    BLOCKS = bfirst.shape[1] - 1
    LEAD = GROUPS0 * TPG0
    ROWS = TPB * WT
    ZC = TILES * WT
    ZP = ZC + (-ZC) % 4
    NIOTA = consts.shape[1] - P - 6
    RUNS = [(low, min(low + RUN, TILES)) for low in range(0, TILES, RUN)]
    assert BLOCKS % 4 == 0 and GROUPS0 == BLOCKS // 2 + 2 and ALLT >= max(LEAD + (BLOCKS + 1) * TPB, GROUPS * TPG)
    assert GROUPS0 % 2 == 0 and TPB % TPR == 0 and ZP <= 512 and ROWS <= P and NIOTA >= max(ZP, P, WB)
    LEFT = GROUPS // 2 - 1 - (CHUNKS - 1) * STRIDE // 2
    assert CHUNKS % 2 == 1 and CHUNKS >= 5 and STRIDE >= 4 and LEFT >= 1
    assert D == P and TILES % RING == 0 and GROUPS % 2 == 0 and sum(CH) == TPG and TAIL > 0

    with ExitStack() as ctx:
        def sb(name, shape, dt):
            return ctx.enter_context(nc.sbuf_tensor(name, shape, dt))

        def sem(name):
            return ctx.enter_context(nc.semaphore(name))

        table0 = nc.dram_tensor("table0", (TILES * P, 2 * D), F16, kind="Internal").ap()
        table1 = nc.dram_tensor("table1", (TILES * P, D), F32, kind="Internal").ap()

        xs = sb("xs", [P, TILES, D], F32)
        hs = sb("hs", [P, TILES, D], F32)
        spare = hs[:, :, :].rearrange("p t d -> p (t d)")
        G0W, O0W = 2 * TPG0 * D, TPG0 * W0 // 2
        gath0 = spare[:, 0:G0W].bitcast(F16).rearrange("p (j t k d) -> p j t k d", j=2, t=TPG0, k=2)
        onehot0 = spare[:, G0W:G0W + 2 * O0W].bitcast(F16).rearrange("p (j w t) -> p j w t", j=2, w=W0)
        assert G0W + 2 * O0W <= TILES * D
        accT = sb("accT", [P, NCOL], F32)
        cntT = sb("cntT", [P, NCOL], F32)
        WORDS = max((TPB * (ZP + P) + 2 * TILES * ROWS) // 2,
                    (2 * GATHERED + TPG) * D + TPG * W + TPG * P // 2 + 2 * TPG * P)
        work = sb("work", [P, WORDS], F32)
        used = [0]

        def carve(words):
            used[0] += words
            return work[:, used[0] - words:used[0]]

        zhot = carve(TPB * ZP // 2).bitcast(F16).rearrange("p (t z) -> p t z", t=TPB)
        lohot = carve(TPB * P // 2).bitcast(F16).rearrange("p (g l t) -> p g l t", l=P, t=TPR)
        adj = carve(TILES * ROWS).bitcast(F16).rearrange("p (j h r) -> p j h r", j=2, h=TILES)
        used[0] = 0
        turned = carve(TILES * 32).rearrange("p (t r) -> p t r", t=TILES)
        used[0] = 0
        gath = carve(2 * GATHERED * D).rearrange("p (j t d) -> p j t d", j=2, t=GATHERED)
        msg = carve(TPG * D).rearrange("p (t d) -> p t d", t=TPG)
        onehot = carve(TPG * W).rearrange("p (t w) -> p t w", t=TPG)
        typehot = carve(TPG * P // 2)[0:K3].bitcast(BF16).rearrange("p (t e) -> p t e", t=TPG)
        types = carve(2 * TPG * P)[0:K3].bitcast(I32).rearrange("p (j e) -> p j e", j=2)
        idxb = sb("idxb", [P, 2, TPG0], I32)
        dst_i = sb("dst_i", [P, ALLT], I32)
        code = dst_i[:, :].bitcast(F32)
        src_lo = sb("src_lo", [P, ALLT], F16)
        cols = sb("cols", [P, 2, TPB], F32)
        h_hi = sb("h_hi", [P, TILES, D + 1], F16)
        h_lo = sb("h_lo", [P, TILES, D], F16)
        at_cnt = [0]

        def from_cnt(words):
            at_cnt[0] += words
            assert at_cnt[0] <= NCOL
            return cntT[:, at_cnt[0] - words:at_cnt[0]]

        st_a, st_b, st_h, st_t = (from_cnt(RING * D).rearrange("p (j d) -> p j d", j=RING) for _ in range(4))
        st_sums = (st_a, st_b)
        node_id = from_cnt(RUN * P // 2).bitcast(F16).rearrange("p (h e) -> p h e", h=RUN)
        src_rel = from_cnt(len(RUNS) * P // 2).bitcast(F16).rearrange("p (r e) -> p r e", e=P)
        pick_src = from_cnt(2 * P).bitcast(I32).rearrange("p (j e) -> p j e", j=2)
        picked, picked_t = from_cnt(P), from_cnt(P)
        st_o = from_cnt(RING * D).rearrange("p (j d) -> p j d", j=RING)
        picks_all = sb("picks", [P, TILES * P // 2], F32)
        picks = picks_all[:, :].bitcast(F16).rearrange("p (t e) -> p t e", t=TILES)
        at_pick = [0]

        def from_picks(words):
            at_pick[0] += words
            assert at_pick[0] <= TILES * P // 2
            return picks_all[:, at_pick[0] - words:at_pick[0]]

        iota16 = sb("iota16", [P, ZP], F16)
        iota_run = from_picks(P * TPR // 2).bitcast(F16).rearrange("p (l t) -> p l t", l=P)
        dst_r0 = from_picks(LEAD // 2).bitcast(F16).rearrange("p (g t) -> p g t", t=TPG0)
        iota_win = from_picks(W0 * TPG0 // 2).bitcast(F16).rearrange("p (w t) -> p w t", w=W0)
        sums = sb("sums", [ROWS, D + 1], F32)
        place = from_picks(2 * WB)[0:ROWS].rearrange("p (j w) -> p j w", j=2)
        vrow = sb("vrow", [ROWS, BLOCKS + 1], F32)
        bfirst_i = sb("bfirst_i", [P, BLOCKS + 1], I32)
        dst_r = sb("dst_r", [P, GROUPS, TPG], F32)
        dcur = sb("dcur", [P, TPG], F32)
        gfirst_i = sb("gfirst_i", [P, GROUPS], I32)
        glast_i = sb("glast_i", [1, GROUPS], I32)
        gfirst0_i = sb("gfirst0_i", [P, GROUPS0], I32)
        glast0_i = sb("glast0_i", [1, GROUPS0], I32)
        stats = from_picks(TILES * 6).rearrange("p (t k) -> p t k", k=6)
        cstats = sb("cstats", [P, RING, 6], F32)
        small = from_picks(6 * TILES).rearrange("p (k t) -> p k t", k=6)
        rstd0 = sb("rstd0", [P, TILES], F32)
        nb0 = sb("nb0", [P, TILES], F32)
        csmall = sb("csmall", [P, 6, RING], F32)
        rstd1 = sb("rstd1", [P, RING], F32)
        nb1 = sb("nb1", [P, RING], F32)
        kc = sb("kc", [P, consts.shape[1]], F32)
        scale_c = sb("scale_c", [P, 1], F32)
        ones16 = sb("ones16", [P, P], F16)
        rcnt = sb("rcnt", [P, TILES], F32)
        crcnt = sb("crcnt", [P, 2, RING], F32)
        w0 = sb("w0", [P, D], F32)
        wx = sb("wx", [P, D], F32)
        wu = sb("wu", [P, D], F32)
        emb_s = sb("emb_s", [embt.shape[0], K3], F32)
        wet_s = sb("wet_s", [wet.shape[0], D], F32)
        rows = sb("rows", [P, 5, D], F32)
        cmat = sb("cmat", [K3, 3, D], F32)
        cpart = sb("cpart", [K3, 3, D], BF16)
        csel = sb("csel", [K3, D], BF16)
        viol = sb("viol", [P, 11], F32)
        dmm = sb("dmm", [P, 4], F32)
        vmax = sb("vmax", [P, 2], F32)
        flag = sb("flag", [P, 1], I32)
        epsc = sb("epsc", [P, 2], F32)
        ends_i = sb("ends_i", [1, 2], I32)

        ident = kc[:, 0:P]
        KI = P + NIOTA
        b0r, msgbr, updbr, lngr, lnbr = (rows[:, k, :] for k in range(5))
        used[0] = 0
        chk_a_all = carve(ALLT).bitcast(I32)
        chk_a = chk_a_all[:, 0:FR]
        chk_b = carve(ALLT).bitcast(I32)[:, 0:FR]
        spans = carve(ALLT)
        chk_d = spans[:, 0:FR]
        src_i = carve(ALLT).bitcast(I32)
        tfirst_i = carve(ALLT).bitcast(I32)
        tends_i = carve(2 * tlast_p.shape[1]).bitcast(I32).rearrange("p (k t) -> p k t", k=2)
        tail = carve(3 * TAIL)
        tail_a, tail_b = (tail[0:1, k * TAIL:(k + 1) * TAIL].bitcast(I32) for k in range(2))
        tail_d = tail[0:1, 2 * TAIL:3 * TAIL]
        blast_i = carve(BLOCKS + 1).bitcast(I32)[0:1, :]
        trep_i = carve(BLOCKS + 1).bitcast(I32)[0:ROWS, :]
        assert used[0] <= WORDS

        ps = ctx.enter_context(nc.psum_tensor("ps", [P, 8, 512], F32))

        def slot(bank, j):
            return ps[:, bank + j // 4, (j % 4) * P:(j % 4 + 1) * P]

        def bank_full(j):
            return 4 if j < 4 else RING

        def two_banks(bank, tiles_of, body):
            for k, (low, high) in enumerate(((0, 4), (4, RING))):
                body(k, tiles_of[:, low:high, :], ps[:, bank + k, 0:(high - low) * P].rearrange("p (j d) -> p j d", d=P))

        psG, psGT = ps[:, 7, 0:P], ps[:, 7, P:2 * P]
        psA = ps[:, 6, 0:W]
        psN = ps[:, 7, 0:W]

        def window_banks(j):
            return ps[:, 6 + j, 2 * WB:2 * WB + W0], ps[:, 6 + j, 2 * WB + W0:2 * WB + 2 * W0]

        s_x = [sem(f"s_x{k}") for k in range(2)]
        s_in = sem("s_in")
        s_chk = sem("s_chk")
        s_pad = sem("s_pad")
        s_zero = sem("s_zero")
        s_dve = sem("s_dve")
        s_viol = sem("s_viol")
        s_vmax = sem("s_vmax")
        s_flag = sem("s_flag")
        s_cps0 = sem("s_cps0")
        s_csel = sem("s_csel")
        s_var0 = sem("s_var0")
        s_std0 = sem("s_std0")
        s_nb0 = sem("s_nb0")
        s_h0 = sem("s_h0")
        s_tab = [sem(f"s_tab_l{l}") for l in range(2)]
        s_idx = [[sem(f"s_idx{l}{j}") for j in range(2)] for l in range(2)]
        s_gath = [[sem(f"s_gath{l}{j}") for j in range(2)] for l in range(2)]
        s_gfree = [sem(f"s_gfree{l}") for l in range(2)]
        s_typ = [sem(f"s_typ{j}") for j in range(2)]
        s_toh = sem("s_toh")
        s_cps = sem("s_cps")
        s_msg = sem("s_msg")
        s_relu = sem("s_relu")
        s_oh = [sem(f"s_oh{l}") for l in range(2)]
        s_agg = [sem(f"s_agg{l}") for l in range(2)]
        s_acc = [sem(f"s_acc_l{l}") for l in range(2)]
        s_rcnt = [sem(f"s_rcnt_l{l}") for l in range(2)]
        s_recip = [sem(f"s_recip{l}") for l in range(2)]
        s_xl = sem("s_xl")
        s_h1hi = sem("s_h1hi")
        s_h1lo = sem("s_h1lo")
        s_psrc = [sem(f"s_psrc{j}") for j in range(2)]
        s_rel = sem("s_rel")
        s_picks = sem("s_picks")
        s_picked = sem("s_picked")
        s_pickc = sem("s_pickc")
        s_turn = sem("s_turn")
        s_turnc = sem("s_turnc")
        s_turned = sem("s_turned")
        s_hst = sem("s_hst")
        s_hnT = sem("s_hnT")
        s_st = [sem(f"s_st{l}") for l in range(2)]
        s_y = [sem(f"s_y{l}") for l in range(2)]
        s_x1 = [sem(f"s_x1_l{l}") for l in range(2)]
        s_var = [sem(f"s_var_l{l}") for l in range(2)]
        s_std = [sem(f"s_std_l{l}") for l in range(2)]
        s_nb = [sem(f"s_nb_l{l}") for l in range(2)]
        s_h1 = sem("s_h1")
        s_keep = sem("s_keep")
        s_hT = sem("s_hT")
        s_hTs = sem("s_hTs")
        s_p = sem("s_p")
        s_ps = sem("s_ps")
        s_z = sem("s_z")
        s_zg = sem("s_zg")
        s_fin = sem("s_fin")
        s_out = sem("s_out")
        s_bn0 = sem("s_bn0")
        s_bn = [sem(f"s_bn_l{l}") for l in range(2)]
        s_step = [sem(f"s_step{l}") for l in range(2)]
        s_dcur = [sem(f"s_dcur{l}") for l in range(2)]
        s_none = sem("s_none")
        s_xb = sem("s_xb")
        s_ones16 = sem("s_ones16")
        s_prep = sem("s_prep")
        s_hhi = sem("s_hhi")
        s_hlo = sem("s_hlo")
        s_cols = sem("s_cols")
        s_zhot = sem("s_zhot")
        s_build = sem("s_build")
        s_evac = sem("s_evac")
        s_dense = sem("s_dense")
        s_sums = sem("s_sums")
        s_place = sem("s_place")
        s_merge = sem("s_merge")
        s_gacc = sem("s_gacc")
        s_dacc = sem("s_dacc")
        s_apart = sem("s_apart")

        NIN = 25
        PARTS = ((0, (CHUNKS + 1) // 2), ((CHUNKS + 1) // 2, CHUNKS))
        MID = PARTS[0][1] * RING
        block = ctx.enter_context(nc.Block())

        def apart(eng):
            eng.sem_inc(s_apart, 1)

        def pairs(eng, body, groups=GROUPS):
            for j in range(2):
                body(j, j, True)
            with eng.Fori(1, groups // 2) as i:
                for j in range(2):
                    body(i * 2 + j, j, False)

        def blocks(eng, body):
            for b in range(4):
                body(b, b % 2, True, b > 0, b > 1, False, b - 2 if b > 1 else None, b % 2)
            with eng.Fori(1, BLOCKS // 4) as i:
                for k in range(4):
                    body(i * 4 + k, k % 2, True, True, True, True, i * 2 + k // 2 if k % 2 else None, k // 2)
            body(BLOCKS, 0, False, True, True, True, BLOCKS // 2, 0)
            body(BLOCKS + 1, 1, False, False, True, True, BLOCKS // 2 + 1, 1)

        def chunks(eng, body):
            body(0, 0, True, False)
            with eng.Fori(0, (CHUNKS - 3) // 2) as i:
                body(i * 2 + 1, 1, False, False)
                body(i * 2 + 2, 0, False, False)
            body(CHUNKS - 2, 1, False, False)
            body(CHUNKS - 1, 0, False, True)

        def groups_and_chunks(eng, group, start, go_on, finish):
            for j in range(2):
                group(j, j, True)
            with eng.Fori(0, CHUNKS - 1) as c:
                if STRIDE > 4:
                    with eng.Fori(0, STRIDE // 2 - 2) as i:
                        for j in range(2):
                            group(c * STRIDE + i * 2 + (2 + j), j, False)
                for k, step in enumerate((None, start, go_on, finish)):
                    group(c * STRIDE + (STRIDE - 2 + k), k % 2, False)
                    if step:
                        step(c)
            if LEFT > 1:
                with eng.Fori(0, LEFT - 1) as i:
                    for j in range(2):
                        group(i * 2 + ((CHUNKS - 1) * STRIDE + 2 + j), j, False)
            group(GROUPS - 2, 0, False, ahead=1)
            group(GROUPS - 1, 1, False, ahead=0)

        @block.sync
        def _(sp):
            sp.dma_start(xs[:, 0:MID, :], x[0:MID * P, :].rearrange("(t p) d -> p t d", p=P)).then_inc(s_x[0], 16)
            sp.dma_start(xs[:, MID:TILES - 1, :],
                         x[MID * P:(TILES - 1) * P, :].rearrange("(t p) d -> p t d", p=P)).then_inc(s_x[1], 16)
            sp.wait_ge(s_pad, 1)
            sp.dma_start(xs[0:LASTROWS, TILES - 1, :], x[(TILES - 1) * P:N, :]).then_inc(s_x[1], 16)
            sp.dma_start(chk_a, dst_flat[0:FR * P].rearrange("(p n) -> p n", p=P)).then_inc(s_chk, 16)
            sp.dma_start(chk_b, dst_flat[1:FR * P + 1].rearrange("(p n) -> p n", p=P)).then_inc(s_chk, 16)
            sp.dma_start(tail_a, dst_flat[None, FR * P:n_edges - 1]).then_inc(s_chk, 16)
            sp.dma_start(tail_b, dst_flat[None, FR * P + 1:n_edges]).then_inc(s_chk, 16)
            sp.dma_start(ends_i[:, 0:1], dst_flat[None, 0:1]).then_inc(s_chk, 16)
            sp.dma_start(ends_i[:, 1:2], dst_flat[None, n_edges - 1:n_edges]).then_inc(s_chk, 16)
            loads = [(kc[:, :], consts), (w0[:, :], w0t), (wx[:, :], wxt), (wu[:, :], updt),
                     (wet_s[:, :], wet), (dst_i[:, :], dst_t), (src_i, src_t),
                     (tfirst_i, tfirst.to_broadcast([P, ALLT])), (tends_i[:, 0, :], tfirst_p),
                     (tends_i[:, 1, :], tlast_p), (blast_i, blast), (trep_i, trep),
                     (bfirst_i[:, :], bfirst.to_broadcast([P, BLOCKS + 1])),
                     (gfirst_i[:, :], gfirst.to_broadcast([P, GROUPS])),
                     (glast_i[:, :], glast), (gfirst0_i[:, :], gfirst0.to_broadcast([P, GROUPS0])),
                     (glast0_i[:, :], glast0)]
            loads += [(emb_s[:, k * NT:(k + 1) * NT], embt) for k in range(3)]
            loads += [(r, v.to_broadcast([P, D])) for r, v in
                      zip((b0r, msgbr, updbr, lngr, lnbr), (b0, msgb, updb, lng, lnb))]
            assert len(loads) == NIN
            for to, of in loads:
                sp.dma_start(to, of).then_inc(s_in, 16)

            t0_hi, t0_lo = (table0[:, k * D:(k + 1) * D].rearrange("(c j p) d -> c p j d", j=RING, p=P)
                            for k in range(2))
            with sp.Fori(0, CHUNKS) as c:
                sp.wait_ge(s_hhi, c + 1)
                sp.dma_start(t0_hi[c], h_hi[:, bass.ds(c * RING, RING), 0:D]).then_inc(s_tab[0], 16)
                sp.wait_ge(s_hlo, c + 1)
                sp.dma_start(t0_lo[c], h_lo[:, bass.ds(c * RING, RING), :]).then_inc(s_tab[0], 16)

            def load_indices(l, n, j, first, indices, size):
                if not first:
                    sp.wait_ge(s_gath[l][j], (n - j) * (8 * size))
                sp.dma_start(idxb[:, j, 0:size], indices[n, :, 0:size]).then_inc(s_idx[l][j], 16)

            def load_edges(n, j, first):
                load_indices(1, n, j, first, idx_g, GATHERED)
                if j or not first:
                    sp.wait_ge(s_toh, n)
                load_types(n + 1, 1 - j)
                sp.wait_ge(s_rel, (n + 1) * len(RUNS))
                load_pick(n + 2, j)

            def load_types(n, j):
                sp.dma_start(types[:, j, :], types_g[n].to_broadcast([K3, TPG * P])).then_inc(s_typ[j], 16)

            def load_pick(n, j):
                sp.dma_start(pick_src[:, j, :], pick_g[n].to_broadcast([P, P])).then_inc(s_psrc[j], 16)

            sp.wait_ge(s_flag, 1)
            flag_sp = sp.value_load(flag[0:1, 0:1], min_val=0, max_val=1)
            with sp.If(flag_sp == 0):
                pairs(sp, lambda n, j, first: load_indices(0, n, j, first, idx0_g, TPG0), GROUPS0)
            with sp.Else():
                pairs(sp, lambda n, j, first: load_indices(0, n, j, first, idx_g, TPG))
            t1 = table1.rearrange("(c j p) d -> c p j d", j=RING, p=P)
            with sp.Fori(0, CHUNKS) as c:
                sp.wait_ge(s_ps, c * 2 + 2)
                sp.dma_start(t1[c], st_o).then_inc(s_tab[1], 16)
            sp.wait_ge(s_turned, 4)
            load_pick(0, 0)
            load_types(0, 0)
            load_pick(1, 1)
            pairs(sp, load_edges)

            sp.wait_ge(s_typ[0], (GROUPS // 2 + 1) * 16)
            for j in range(2):
                sp.wait_ge(s_psrc[j], (GROUPS // 2 + 1) * 16)
            sp.wait_ge(s_out, (CHUNKS + 1) * 16)

        @block.gpsimd
        def _(pool):
            nc.gpsimd.memset(xs[:, TILES - 1, :], 0.0).then_inc(s_pad, 1)
            nc.gpsimd.memset(accT[:, :], 0.0).then_inc(s_acc[0], 1)
            nc.gpsimd.memset(cntT[:, :], 0.0).then_inc(s_zero, 1)
            pool.wait_ge(s_zero, 1)
            pool.wait_ge(s_acc[0], 1)
            pool.sem_inc(s_dacc, 1)
            nc.gpsimd.memset(ones16[:, :], 1.0).then_inc(s_zero, 1)
            nc.gpsimd.memset(scale_c[:, :], SCALE).then_inc(s_ones16, 1)
            nc.gpsimd.memset(h_hi[:, :, D:D + 1], SCALE).then_inc(s_ones16, 1)
            def gather(l, j, size, to, table):
                apart(pool)
                for k in range(size):
                    pool.indirect_dma_start(
                        to[:, k], None, table,
                        bass.IndirectOffsetOnAxis(ap=idxb[:, j, k:k + 1].bitcast(U32), axis=0),
                    ).then_inc(s_gath[l][j], 16)

            def gather0(n, j, first, size, used):
                pool.wait_ge(s_idx[0][j], (n - j) * 8 + 16)
                if not first:
                    pool.wait_ge(used, n - 1)
                gather(0, j, size, gath0[:, j].rearrange("p t k d -> p t (k d)"), table0)

            def gather1(n, j, first):
                pool.wait_ge(s_idx[1][j], (n - j) * 8 + 16)
                if not first:
                    pool.wait_ge(s_msg, (n - 1) * len(CH))
                gather(1, j, GATHERED, gath[:, j], table1)

            def second_parts(low, high):
                with pool.Fori(low, high) as c:
                    some = bass.ds(c * RING, RING)
                    pool.wait_ge(s_hhi, c + 1)
                    nc.gpsimd.tensor_tensor(h_lo[:, some, :], hs[:, some, :], h_hi[:, some, 0:D],
                                            ALU.subtract).then_inc(s_hlo, 1)

            second_parts(*PARTS[0])
            pool.wait_ge(s_viol, 1)
            nc.gpsimd.partition_all_reduce(vmax[:, 1:2], vmax[:, 0:1], P, RMAX).then_inc(s_vmax, 1)
            second_parts(*PARTS[1])
            pool.wait_ge(s_hlo, CHUNKS)
            pool.wait_ge(s_tab[0], 2 * CHUNKS * 16)
            pool.wait_ge(s_flag, 1)
            flag_pool = pool.value_load(flag[0:1, 0:1], min_val=0, max_val=1)
            with pool.If(flag_pool == 0):
                pairs(pool, lambda n, j, first: gather0(n, j, first, TPG0, s_agg[0]), GROUPS0)
            with pool.Else():
                pairs(pool, lambda n, j, first: gather0(n, j, first, TPG, s_gfree[0]))

            pool.wait_ge(s_in, 16 * NIN)
            pool.wait_ge(s_h0, TILES)
            with pool.Fori(0, CHUNKS) as c:
                some = bass.ds(c * RING, RING)
                nc.gpsimd.tensor_tensor(xs[:, some, :], xs[:, some, :], rows[:, 0:1, :].to_broadcast([P, RING, D]),
                                        ALU.add).then_inc(s_xb, 1)

            pool.wait_ge(s_ones16, 2)
            with pool.Fori(0, CHUNKS) as c:
                pool.wait_ge(s_h1, c * RING + RING)
                nc.gpsimd.tensor_tensor(h_hi[:, bass.ds(c * RING, RING), 0:D], st_h,
                                        scale_c[:, None, :].to_broadcast([P, RING, D]), ALU.mult).then_inc(s_h1hi, 1)
                nc.gpsimd.tensor_tensor(hs[:, bass.ds(c * RING, RING), :], st_h,
                                        rows[:, 2:3, :].to_broadcast([P, RING, D]),
                                        ALU.add).then_inc(s_keep, 1)
            pool.wait_ge(s_tab[1], 16 * CHUNKS)
            pairs(pool, gather1)

        @block.scalar
        def _(act):
            for k, (low, high) in enumerate(PARTS):
                tiles_of = slice(low * RING, high * RING)
                act.wait_ge(s_var0, k + 1)
                nc.scalar.activation(small[:, 5, tiles_of], small[:, 4, tiles_of], ACT.Sqrt, bias=epsc[:, 1:2],
                                     scale=1.0 / (D * SCALE * SCALE)).then_inc(s_std0, 1)
                act.wait_ge(s_nb0, k + 1)
                with act.Fori(low, high) as c:
                    for j in range(RING):
                        t = c * RING + j
                        nc.scalar.activation(hs[:, t, :], xs[:, t, :], ACT.Relu, bias=nb0[:, bass.ds(t, 1)],
                                             scale=rstd0[:, bass.ds(t, 1)]).then_inc(s_h0, 1)
                    act.wait_ge(s_h0, c * RING + RING)
                    some = bass.ds(c * RING, RING)
                    nc.scalar.activation(h_hi[:, some, 0:D], hs[:, some, :], ACT.Copy).then_inc(s_hhi, 1)
            act.wait_ge(s_flag, 1)
            flag_act = act.value_load(flag[0:1, 0:1], min_val=0, max_val=1)

            def copy_out(b, j, build, dense, merge, steady, group, gj):
                if build:
                    if merge:
                        act.wait_ge(s_dense, b - 1)
                    for t in range(TPB):
                        act.wait_ge(s_build, b * TPB + (t + 1))
                        nc.scalar.activation(adj[:, j, :, t * WT:(t + 1) * WT],
                                             ps[:, (j * TPB + t) % 4, 0:ZC].rearrange("p (h w) -> p h w", w=WT),
                                             ACT.Copy).then_inc(s_evac, 1)
                if dense:
                    act.wait_ge(s_dense, b)
                    if merge:
                        act.wait_ge(s_merge, b - 1)
                    nc.scalar.activation(sums[:, :], ps[0:ROWS, 5 - j, 0:D + 1], ACT.Copy,
                                         scale=1.0 / SCALE).then_inc(s_sums, 1)

            with act.If(flag_act == 0):
                blocks(act, copy_out)

            def table_rows(c, j, first, last):
                act.wait_ge(s_var[0], c + 1)
                nc.scalar.activation(csmall[:, 5, :], csmall[:, 4, :], ACT.Sqrt, bias=epsc[:, 0:1],
                                     scale=1.0 / D).then_inc(s_std[0], 1)
                act.wait_ge(s_nb[0], c + 1)
                if not first:
                    act.wait_ge(s_keep, c)
                    act.wait_ge(s_hT, c * 2)
                    act.wait_ge(s_h1lo, c)
                for t in range(RING):
                    nc.scalar.activation(st_h[:, t, :], xs[:, c * RING + t, :], ACT.Relu, bias=nb1[:, t:t + 1],
                                         scale=rstd1[:, t:t + 1]).then_inc(s_h1, 1)

                def copy_transposed(k, to, of):
                    act.wait_ge(s_hT, c * 2 + (k + 1))
                    nc.scalar.activation(to, of, ACT.Copy).then_inc(s_hTs, 1)

                def copy_rows(k, to, of):
                    act.wait_ge(s_p, c * 2 + (k + 1))
                    nc.scalar.activation(to, of, ACT.Copy).then_inc(s_ps, 1)

                two_banks(2, st_t, copy_transposed)
                if not first:
                    act.wait_ge(s_tab[1], c * 16)
                two_banks(4, st_o, copy_rows)

            chunks(act, table_rows)
            act.wait_ge(s_tab[1], CHUNKS * 16)

            def relu_messages(n, j, first, ahead=2):
                for c, w in enumerate(CH):
                    act.wait_ge(s_msg, n * len(CH) + (c + 1))
                    m = msg[:, SLOT0[c]:SLOT0[c] + w, :]
                    nc.scalar.activation(m, m, ACT.Relu).then_inc(s_relu, 1)
                if ahead:
                    copy_picked(n + 1, False)

            def copy_picked(n, first):
                if not first:
                    act.wait_ge(s_cps, n * len(CH))
                act.wait_ge(s_picked, n + 1)
                nc.scalar.activation(picked, psG, ACT.Copy, scale=1.0 / SCALE).then_inc(s_pickc, 1)
                act.wait_ge(s_turn, n + 1)
                nc.scalar.activation(picked_t, psGT, ACT.Copy).then_inc(s_turnc, 1)

            oc = out[0:(CHUNKS - 1) * RING * P, :].rearrange("(c j p) d -> c p j d", j=RING, p=P)

            def deviations(c):
                act.wait_ge(s_var[1], c + 1)
                nc.scalar.activation(csmall[:, 5, :], csmall[:, 4, :], ACT.Sqrt, bias=epsc[:, 0:1],
                                     scale=1.0 / D).then_inc(s_std[1], 1)

            def normalise(c):
                act.wait_ge(s_nb[1], c + 1)
                for t in range(RING):
                    nc.scalar.activation(st_h[:, t, :], hs[:, c * RING + t, :], ACT.Identity, bias=nb1[:, t:t + 1],
                                         scale=rstd1[:, t:t + 1]).then_inc(s_z, 1)
                act.wait_ge(s_fin, c + 1)

            def store(c):
                act.dma_start(oc[c], st_o).then_inc(s_out, 16)
                act.wait_ge(s_out, c * 16 + 16)

            def finish(c):
                normalise(c)
                store(c)

            copy_picked(0, True)
            with act.If(flag_act == 0):
                groups_and_chunks(act, relu_messages, None, deviations, finish)
            with act.Else():
                pairs(act, relu_messages)
                with act.Fori(0, CHUNKS - 1) as c:
                    deviations(c)
                    finish(c)
            deviations(CHUNKS - 1)
            normalise(CHUNKS - 1)
            at = (CHUNKS - 1) * RING * P
            act.dma_start(out[at:at + (RING - 1) * P, :].rearrange("(j p) d -> p j d", p=P),
                          st_o[:, 0:RING - 1, :]).then_inc(s_out, 16)
            act.dma_start(out[(TILES - 1) * P:N, :], st_o[0:LASTROWS, RING - 1, :]).then_inc(s_out, 16)

        @block.tensor
        def _(pe):
            pe.wait_ge(s_zero, 2)
            pe.wait_ge(s_flag, 1)
            flag_pe = pe.value_load(flag[0:1, 0:1], min_val=0, max_val=1)

            def type_terms(n, first):
                pe.wait_ge(s_toh, n + 1)
                if not first:
                    pe.wait_ge(s_msg, n * len(CH))
                for c, w in enumerate(CH):
                    picked_one = c == len(CH) - 1
                    low = SLOT0[c] - SLOT0[BANK.index(BANK[c])]
                    for k in range(w):
                        last = nc.tensor.matmul(ps[:, BANK[c], (low + k) * P:(low + k + 1) * P],
                                                typehot[:, SLOT0[c] + k, :], csel[:, :],
                                                start=True, stop=not picked_one)
                    if picked_one:
                        pe.wait_ge(s_turnc, n + 1)
                        last = nc.tensor.matmul(ps[:, BANK[c], low * P:(low + 1) * P], picked_t, wx[:, :],
                                                start=False, stop=True)
                    last.then_inc(s_cps, 1)

            def pick_rows(n, first):
                if not first:
                    pe.wait_ge(s_turnc, n)
                for r, (low, high) in enumerate(RUNS):
                    pe.wait_ge(s_picks, n * len(RUNS) + (r + 1))
                    for h in range(low, high):
                        nc.tensor.matmul(psG, picks[:, h, :], h_hi[:, h, 0:D], start=(h == 0), stop=False)
                        last = nc.tensor.matmul(psG, picks[:, h, :], h_lo[:, h, :], start=False,
                                                stop=(h == TILES - 1))
                last.then_inc(s_picked, 1)

            def turn_picked(n):
                pe.wait_ge(s_pickc, n + 1)
                nc.tensor.transpose(psGT, picked, ident).then_inc(s_turn, 1)

            def window_sums0(j, size, width, sums_to, counts_to):
                for k in range(size):
                    for part in range(2):
                        nc.tensor.matmul(sums_to, gath0[:, j, k, part, :], onehot0[:, j, 0:width, k],
                                         start=(k + part == 0), stop=(k == size - 1 and part == 1))
                for k in range(size):
                    last = nc.tensor.matmul(counts_to, ones16[:, :], onehot0[:, j, 0:width, k],
                                            start=(k == 0), stop=(k == size - 1))
                last.then_inc(s_agg[0], 1)

            def window_sums1(n, q):
                pe.wait_ge(s_oh[1], q + 1)
                for k in range(TPG):
                    if k in SLOT0:
                        pe.wait_ge(s_relu, n * len(CH) + (SLOT0.index(k) + 1))
                    last = nc.tensor.matmul(psA, msg[:, k, :], onehot[:, k, :], start=(k == 0), stop=(k == TPG - 1))
                last.then_inc(s_agg[1], 1)

            def dense_block(b, j, build, dense, merge, steady, group, gj):
                if dense:
                    if not steady and b == 1:
                        pe.wait_ge(s_ones16, 2)
                        pe.wait_ge(s_hhi, CHUNKS)
                        pe.wait_ge(s_hlo, CHUNKS)
                    pe.wait_ge(s_evac, b * TPB)
                    if steady or b == 3:
                        pe.wait_ge(s_sums, b - 2)
                acc = ps[0:ROWS, 5 - j, :]
                for t in range(TPB):
                    if build:
                        pe.wait_ge(s_zhot, b * TPB + (t + 1))
                        if dense or t >= 4:
                            pe.wait_ge(s_evac, b * TPB + (t - 3))
                        nc.tensor.matmul(ps[:, (j * TPB + t) % 4, 0:ZC], lohot[:, t // TPR, :, t % TPR],
                                         zhot[:, t, 0:ZC],
                                         start=True, stop=True).then_inc(s_build, 1)
                    if dense:
                        for h in range(t * TILES // TPB, (t + 1) * TILES // TPB):
                            a = adj[:, 1 - j, h, :]
                            nc.tensor.matmul(acc[:, 0:D + 1], a, h_hi[:, h, :], start=(h == 0), stop=False)
                            last = nc.tensor.matmul(acc[:, 0:D], a, h_lo[:, h, :], start=False, stop=(h == TILES - 1))
                if dense:
                    last.then_inc(s_dense, 1)
                if merge:
                    if steady:
                        pe.wait_ge(s_dacc, b * 2 - 5)
                    if group is not None:
                        pe.wait_ge(s_gath[0][gj], (group - gj) * (8 * TPG0) + 16 * TPG0)
                        pe.wait_ge(s_oh[0], group + 1)
                        window_sums0(gj, TPG0, W0, *window_banks(j))
                    pe.wait_ge(s_sums, b - 1)
                    pe.wait_ge(s_place, b - 1)
                    nc.tensor.matmul(ps[:, 6 + j, 0:WB], sums[:, 0:D], place[:, j, :], start=True, stop=True)
                    nc.tensor.matmul(ps[:, 6 + j, WB:2 * WB], sums[:, D:D + 1].to_broadcast([ROWS, P]),
                                     place[:, j, :], start=True, stop=True).then_inc(s_merge, 1)

            def layer(l):
                def group(n, j, first, windows, ahead=2):
                    if l == 0:
                        pe.wait_ge(s_gath[0][j], (n - j) * (8 * TPG) + 16 * TPG)
                    if windows:
                        apart(pe)
                        with pe.Fori(0, NW) as w:
                            q = n * NW + w
                            if l:
                                window_sums1(n, q)
                            else:
                                pe.wait_ge(s_oh[0], q + 1)
                                window_sums0(j, TPG, W, psA, psN)
                    else:
                        window_sums1(n, n)
                    if l and ahead:
                        turn_picked(n + 1)
                        type_terms(n + 1, False)
                        if ahead == 2:
                            pick_rows(n + 2, False)

                def no_edges(t):
                    pe.wait_ge(s_hst, t + 1)
                    nc.tensor.transpose(slot(0, 0), msg[:, 0, :], ident).then_inc(s_hnT, 1)

                with pe.If(flag_pe == 0):
                    if l:
                        groups_and_chunks(pe, lambda n, j, first, ahead=2: group(n, j, first, False, ahead),
                                          update_products, None, None)
                    else:
                        blocks(pe, dense_block)
                with pe.Else():
                    pairs(pe, lambda n, j, first: group(n, j, first, True))
                    if l == 0:
                        with pe.Fori(0, TILES) as t:
                            no_edges(t)
                    else:
                        with pe.Fori(0, CHUNKS - 1) as c:
                            update_products(c)

            def mean_products(c, j):
                pe.wait_ge(s_st[0], c + 1)
                for t in range(RING):
                    nc.tensor.matmul(slot(6 * j, t), st_sums[j][:, t, :], w0[:, :],
                                     start=True, stop=True).then_inc(s_y[0], 1)

            def node_products(c, j, first, last):
                if first:
                    mean_products(0, 0)
                if not last:
                    mean_products(c + 1, 1 - j)
                if not first:
                    pe.wait_ge(s_hTs, c * 2)
                for t in range(RING):
                    pe.wait_ge(s_h1, c * RING + (t + 1))
                    turn = nc.tensor.transpose(slot(2, t), st_h[:, t, :], ident)
                    if t + 1 == bank_full(t):
                        turn.then_inc(s_hT, 1)
                if not first:
                    pe.wait_ge(s_ps, c * 2)
                for t in range(RING):
                    pe.wait_ge(s_hTs, c * 2 + (1 if t < 4 else 2))
                    product = nc.tensor.matmul(slot(4, t), st_t[:, t, :], wx[:, :], start=True, stop=True)
                    if t + 1 == bank_full(t):
                        product.then_inc(s_p, 1)

            def update_products(c):
                pe.wait_ge(s_st[1], c + 1)
                for t in range(RING):
                    nc.tensor.matmul(slot(4, t), st_a[:, t, :], wu[:, :], start=True, stop=True).then_inc(s_y[1], 1)

            layer(0)
            chunks(pe, node_products)
            pe.wait_ge(s_ps, 2 * CHUNKS)
            pe.wait_ge(s_x1[0], TILES)
            pe.wait_ge(s_h1hi, CHUNKS)
            pe.wait_ge(s_h1lo, CHUNKS)
            pe.wait_ge(s_in, 16 * NIN)
            nc.tensor.matmul(slot(0, 0)[0:K3, :], emb_s[:, :], wet_s[:, :], start=True, stop=True).then_inc(s_cps0, 1)
            pick_rows(0, True)
            turn_picked(0)
            pe.wait_ge(s_csel, 1)
            type_terms(0, True)
            pick_rows(1, False)
            layer(1)
            update_products(CHUNKS - 1)

        @block.vector
        def _(dve):
            chained = [0]

            def chain(ins):
                chained[0] += 1
                ins.then_inc(s_dve, 1)
                dve.wait_ge(s_dve, chained[0])

            def spread(st, sm, step):
                me, qe, mo, qo = (st[:, :, k] for k in (1, 2, 4, 5))
                step(nc.vector.tensor_tensor(sm[:, 0, :], me, mo, ALU.add))
                step(nc.vector.tensor_tensor(sm[:, 1, :], me, mo, ALU.subtract))
                step(nc.vector.tensor_tensor(sm[:, 2, :], qe, qo, ALU.add))
                step(nc.vector.tensor_tensor(sm[:, 3, :], sm[:, 1, :], sm[:, 1, :], ALU.mult))
                return nc.vector.scalar_tensor_tensor(sm[:, 4, :], sm[:, 3, :], D / 4.0, sm[:, 2, :],
                                                      ALU.mult, ALU.add)

            nc.vector.memset(epsc[:, 0:1], EPS)
            nc.vector.memset(epsc[:, 1:2], EPS / (SCALE * SCALE))
            chain(nc.vector.memset(viol[:, :], 0.0))
            for k, (low, high) in enumerate(PARTS):
                tiles_of = slice(low * RING, high * RING)
                dve.wait_ge(s_x[k], 16 * (k + 1))
                with dve.Fori(low, high) as c:
                    for j in range(RING):
                        nc.vector.bn_stats(stats[:, c * RING + j, :], xs[:, c * RING + j, :]).then_inc(s_bn0, 1)
                dve.wait_ge(s_bn0, high * RING)
                part = small[:, :, tiles_of]
                spread(stats[:, tiles_of, :], part, chain).then_inc(s_var0, 1)
                if k == 1:
                    dve.wait_ge(s_chk, 16 * 6)
                    dve.wait_ge(s_in, 16 * NIN)
                    chain(nc.vector.tensor_tensor(chk_d, chk_b, chk_a, ALU.subtract))
                    chain(nc.vector.tensor_tensor(tail_d, tail_b, tail_a, ALU.subtract))
                    chain(nc.vector.tensor_reduce(dmm[:, 0:1], chk_d, AX.X, ALU.max))
                    chain(nc.vector.tensor_reduce(dmm[:, 1:2], chk_d, AX.X, ALU.min))
                dve.wait_ge(s_std0, k + 1)
                chain(nc.vector.reciprocal(rstd0[:, tiles_of], part[:, 5, :]))
                nc.vector.scalar_tensor_tensor(nb0[:, tiles_of], part[:, 0, :], -0.5, rstd0[:, tiles_of],
                                               ALU.mult, ALU.mult).then_inc(s_nb0, 1)

            chain(nc.vector.tensor_reduce(dmm[0:1, 2:3], tail_d, AX.X, ALU.max))
            chain(nc.vector.tensor_reduce(dmm[0:1, 3:4], tail_d, AX.X, ALU.min))
            chain(nc.vector.tensor_scalar(viol[:, 0:1], dmm[:, 0:1], -1.0, None, ALU.add))
            chain(nc.vector.tensor_scalar(viol[:, 1:2], dmm[:, 1:2], -1.0, None, ALU.mult))
            chain(nc.vector.tensor_scalar(viol[0:1, 2:3], dmm[0:1, 2:3], -1.0, None, ALU.add))
            chain(nc.vector.tensor_scalar(viol[0:1, 3:4], dmm[0:1, 3:4], -1.0, None, ALU.mult))
            chain(nc.vector.tensor_copy(viol[0:1, 4:5], ends_i[0:1, 0:1]))
            chain(nc.vector.tensor_scalar(viol[0:1, 5:6], ends_i[0:1, 1:2], -1.0, float(N - 1), ALU.mult, ALU.add))
            for k, (late, early, width) in enumerate(((glast_i[0:1, :], gfirst_i[0:1, :], W),
                                                      (glast0_i[0:1, :], gfirst0_i[0:1, :], W0),
                                                      (blast_i, bfirst_i[0:1, :], WB),
                                                      (tends_i[:, 1, :], tends_i[:, 0, :], WT))):
                span = spans[0:late.shape[0], 0:late.shape[1]]
                v = viol[0:late.shape[0], 6 + k:7 + k]
                chain(nc.vector.tensor_tensor(span, late, early, ALU.subtract))
                chain(nc.vector.tensor_reduce(v, span, AX.X, ALU.max))
                chain(nc.vector.tensor_scalar(v, v, -float(width - 1), None, ALU.add))
            ends_of = spans[0:1, 0:CHUNKS - 1]
            chain(nc.vector.scalar_tensor_tensor(
                ends_of, kc[0:1, P + 1:P + CHUNKS], float(RING * P),
                gfirst_i[0:1, STRIDE:STRIDE * (CHUNKS - 1) + 1:STRIDE], ALU.mult, ALU.subtract))
            chain(nc.vector.tensor_reduce(viol[0:1, 10:11], ends_of, AX.X, ALU.max))
            nc.vector.tensor_reduce(vmax[:, 0:1], viol[:, :], AX.X, ALU.max).then_inc(s_viol, 1)
            dve.wait_ge(s_vmax, 1)
            nc.vector.tensor_scalar(flag[:, :], vmax[:, 1:2], 0.0, None, ALU.is_gt).then_inc(s_flag, 1)
            one_window = dmm[:, 0:1]
            chain(nc.vector.tensor_scalar(one_window, vmax[:, 1:2], 0.0, None, ALU.is_le))
            base = spans[:, 0:GROUPS]
            chain(nc.vector.tensor_scalar(base, gfirst_i[:, :], one_window, None, ALU.mult))
            chain(nc.vector.tensor_tensor(dst_r[:, :, :],
                                          dst_i[:, 0:GROUPS * TPG].rearrange("p (g t) -> p g t", t=TPG),
                                          base[:, :, None].to_broadcast([P, GROUPS, TPG]), ALU.subtract))

            src_hi = chk_a_all
            chain(nc.vector.tensor_scalar(src_hi, src_i, 7, None, ALU.logical_shift_right))
            chain(nc.vector.tensor_scalar(src_i, src_i, P - 1, None, ALU.bitwise_and))
            chain(nc.vector.tensor_copy(src_lo[:, :], src_i))
            chain(nc.vector.tensor_tensor(dst_r0, dst_i[:, 0:LEAD].rearrange("p (g t) -> p g t", t=TPG0),
                                          gfirst0_i[:, :, None].to_broadcast([P, GROUPS0, TPG0]), ALU.subtract))
            chain(nc.vector.tensor_tensor(code, dst_i[:, :], tfirst_i, ALU.subtract))
            chain(nc.vector.scalar_tensor_tensor(code, src_hi, float(WT), code, ALU.mult, ALU.add))
            chain(nc.vector.tensor_tensor(vrow[:, :], trep_i, bfirst_i[0:ROWS, :], ALU.subtract))
            chain(nc.vector.tensor_scalar(vrow[:, :], vrow[:, :], kc[0:ROWS, KI + 4:KI + 5], None, ALU.add))
            chain(nc.vector.tensor_copy(iota_run, kc[:, P:2 * P][:, :, None].to_broadcast([P, P, TPR])))
            chain(nc.vector.tensor_copy(iota_win, kc[:, P:P + W0][:, :, None].to_broadcast([P, W0, TPG0])))
            nc.vector.tensor_copy(iota16[:, :], kc[:, P:P + ZP]).then_inc(s_prep, 1)
            dve.wait_ge(s_prep, 1)

            dve.wait_ge(s_zero, 2)
            flag_dve = dve.value_load(flag[0:1, 0:1], min_val=0, max_val=1)

            def columns_of(b, j):
                nc.vector.tensor_copy(cols[:, j, :], code[:, bass.ds(b * TPB + LEAD, TPB)]).then_inc(s_cols, 1)

            def one_hots(b, j, dense):
                dve.wait_ge(s_cols, b + 1)
                for t in range(0, TPB, TPR):
                    if dense:
                        dve.wait_ge(s_build, b * TPB + (t + TPR - TPB))
                    sources = src_lo[:, None, bass.ds(b * TPB + (LEAD + t), TPR)]
                    nc.vector.tensor_tensor(lohot[:, t // TPR], iota_run, sources.to_broadcast([P, P, TPR]),
                                            ALU.is_equal)
                    for u in range(t, t + TPR):
                        nc.vector.tensor_scalar(zhot[:, u, :], iota16[:, :], cols[:, j, u:u + 1], None,
                                                ALU.is_equal).then_inc(s_zhot, 1)
                    if t == TPB // 2 // TPR * TPR:
                        if dense:
                            dve.wait_ge(s_zhot, b * TPB)
                        columns_of(b + 1, 1 - j)

            def load_places(firsts, b, count):
                return nc.values_load_multi_w_load_instructions(
                    firsts[0:1, bass.ds(b, count)], engines=[dve.engine], min_val=0, max_val=N - 1)[1]

            def window_onehot(g, j, first=False):
                if not first:
                    dve.wait_ge(s_agg[0], g - 1)
                nc.vector.tensor_tensor(onehot0[:, j], iota_win,
                                        dst_r0[:, bass.ds(g, 1), :].to_broadcast([P, W0, TPG0]),
                                        ALU.is_equal).then_inc(s_oh[0], 1)

            def add_scaled(total, col, sums_of, factor):
                at = total[:, bass.ds(col, sums_of.shape[-1])]
                return nc.vector.scalar_tensor_tensor(at, sums_of, factor, at, ALU.mult, ALU.add)

            def place_block(b, j):
                nc.vector.tensor_scalar(place[:, j, :], kc[0:ROWS, P:P + WB], vrow[:, bass.ds(b, 1)], None,
                                        ALU.is_equal).then_inc(s_place, 1)

            def add_block(b, j, col, group=None, gcol=None):
                dve.wait_ge(s_merge, b + 1)
                dve.wait_ge(s_dacc, b * 2 + 1)
                if group is not None:
                    w_sums, w_counts = window_banks(j)
                    add_scaled(accT, gcol, w_sums, 1.0 / SCALE).then_inc(s_gacc, 1)
                    add_scaled(cntT, gcol, w_counts, 1.0).then_inc(s_gacc, 1)
                    dve.wait_ge(s_gacc, group * 2 + 2)
                for k, total in enumerate((accT, cntT)):
                    nc.vector.tensor_tensor(total[:, bass.ds(col, WB)], total[:, bass.ds(col, WB)],
                                            ps[:, 6 + j, k * WB:(k + 1) * WB], ALU.add).then_inc(s_dacc, 1)

            def dense_blocks():
                columns_of(0, 0)
                one_hots(0, 0, False)
                one_hots(1, 1, True)
                dve.wait_ge(s_hlo, CHUNKS)
                dve.wait_ge(s_tab[0], 2 * CHUNKS * 16)
                window_onehot(0, 0, True)
                place_block(0, 0)
                one_hots(2, 0, True)
                window_onehot(1, 1, True)
                place_block(1, 1)
                col = load_places(bfirst_i, 0, 1)
                gcol = load_places(gfirst0_i, 0, 1)
                one_hots(3, 1, True)
                add_block(0, 0, col[0], 0, gcol[0])
                place_block(2, 0)
                with dve.Fori(1, BLOCKS // 4) as i:
                    col = load_places(bfirst_i, i * 4 - 3, 4)
                    gcol = load_places(gfirst0_i, i * 2 - 1, 2)
                    for k in range(4):
                        one_hots(i * 4 + k, k % 2, True)
                        if k % 2 == 0:
                            add_block(i * 4 + (k - 3), 1, col[k], i * 2 + (k // 2 - 1), gcol[k // 2])
                            window_onehot(i * 2 + k // 2, k // 2)
                        else:
                            add_block(i * 4 + (k - 3), 0, col[k])
                        place_block(i * 4 + (k - 1), 1 - k % 2)
                col = load_places(bfirst_i, BLOCKS - 3, 1)
                gcol = load_places(gfirst0_i, GROUPS0 - 3, 1)
                add_block(BLOCKS - 3, 1, col[0], GROUPS0 - 3, gcol[0])
                place_block(BLOCKS - 1, 1)
                window_onehot(GROUPS0 - 2, 0)
                window_onehot(GROUPS0 - 1, 1)
                for k in range(2):
                    col = load_places(bfirst_i, BLOCKS - 2 + k, 1)
                    gcol = load_places(gfirst0_i, GROUPS0 - 2 + k, 1)
                    add_block(BLOCKS - 2 + k, k, col[0], GROUPS0 - 2 + k, gcol[0])
                dve.wait_ge(s_dacc, 2 * BLOCKS + 1)

            def make_onehot(l, q, dst, to):
                dve.wait_ge(s_acc[l], q * (2 - l) + 1)
                nc.vector.tensor_tensor(to, kc[:, None, P:P + W].to_broadcast([P, TPG, W]),
                                        dst[:, :, None].to_broadcast([P, TPG, W]), ALU.is_equal).then_inc(s_oh[l], 1)

            def add_window(l, q, col):
                dve.wait_ge(s_agg[l], q + 1)
                if l:
                    nc.vector.tensor_tensor(accT[:, bass.ds(col, W)], accT[:, bass.ds(col, W)], psA,
                                            ALU.add).then_inc(s_acc[1], 1)
                else:
                    add_scaled(accT, col, psA, 1.0 / SCALE).then_inc(s_acc[0], 1)
                    add_scaled(cntT, col, psN, 1.0).then_inc(s_acc[0], 1)

            def pick_sources(n, j, first):
                dve.wait_ge(s_psrc[j], (n - j) * 8 + 16)
                if not first:
                    dve.wait_ge(s_picked, n)
                for r, (low, high) in enumerate(RUNS):
                    nc.vector.tensor_scalar(src_rel[:, r, :], pick_src[:, j, :], -float(low * P), None,
                                            ALU.add).then_inc(s_rel, 1)
                for r, (low, high) in enumerate(RUNS):
                    dve.wait_ge(s_rel, n * len(RUNS) + (r + 1))
                    nc.vector.tensor_tensor(picks[:, low:high, :], node_id[:, 0:high - low, :],
                                            src_rel[:, r:r + 1, :].to_broadcast([P, high - low, P]),
                                            ALU.is_equal).then_inc(s_picks, 1)

            def one_hot_types(n, j):
                dve.wait_ge(s_typ[j], (n - j) * 8 + 16)
                nc.vector.tensor_scalar(typehot[:, :, :].rearrange("k t e -> k (t e)"), types[:, j, :],
                                        kc[0:K3, KI:KI + 1], None, ALU.is_equal).then_inc(s_toh, 1)

            def messages(n, j, ahead=2):
                dve.wait_ge(s_gath[1][j], (n - j) * (8 * GATHERED) + 16 * GATHERED)
                for c, w in enumerate(CH):
                    there = max(k for k in range(len(CH)) if BANK[k] == BANK[c])
                    dve.wait_ge(s_cps, n * len(CH) + (there + 1))
                    low = SLOT0[c] - SLOT0[BANK.index(BANK[c])]
                    terms = ps[:, BANK[c], low * P:(low + w) * P].rearrange("p (t d) -> p t d", d=D)
                    m = msg[:, SLOT0[c]:SLOT0[c] + w, :]
                    if SLOT0[c] < GATHERED:
                        nc.vector.tensor_tensor(m, gath[:, j, SLOT0[c]:SLOT0[c] + w, :], terms,
                                                ALU.add).then_inc(s_msg, 1)
                    else:
                        nc.vector.tensor_copy(m, terms).then_inc(s_msg, 1)
                if ahead:
                    one_hot_types(n + 1, 1 - j)
                if ahead == 2:
                    pick_sources(n + 2, j, False)

            def layer(l):
                def group(n, j, first, ahead=2):
                    make_onehot(1, n, dst_r[:, n, :], onehot[:, :, :])
                    messages(n, j, ahead)
                    col = dve.value_load(gfirst_i[0:1, bass.ds(n, 1)], min_val=0, max_val=N - 1)
                    add_window(1, n, col)

                def group_all_windows(n, j, first):
                    if l:
                        messages(n, j)
                    if j or not first:
                        dve.wait_ge(s_dcur[l], n * (NW + 1))
                    nc.vector.tensor_copy(dcur[:, :], dst_r[:, n, :]).then_inc(s_dcur[l], 1)
                    with dve.Fori(0, NW) as w:
                        q = n * NW + w
                        dve.wait_ge(s_dcur[l], n * (NW + 1) + w + 1)
                        make_onehot(l, q, dcur, onehot[:, :, :] if l else
                                    onehot0[:, j, 0:W, 0:TPG].rearrange("p w t -> p t w"))
                        dve.wait_ge(s_oh[l], q + 1)
                        nc.vector.tensor_scalar(dcur[:, :], dcur[:, :], -float(W), None, ALU.add).then_inc(s_dcur[l], 1)
                        add_window(l, q, w * W)
                    if l == 0:
                        dve.sem_inc(s_gfree[0], 1)

                def no_edges(t):
                    col = bass.ds(t * P, P)
                    h0, none, h0_none = (msg[:, k, :] for k in range(3))
                    nc.vector.tensor_tensor(h0, h_hi[:, t, 0:D], h_lo[:, t, :], ALU.add).then_inc(s_hst, 1)
                    nc.vector.tensor_scalar(none, cntT[:, col], 0.0, None, ALU.is_equal).then_inc(s_none, 1)
                    dve.wait_ge(s_hnT, t + 1)
                    dve.wait_ge(s_none, t * 3 + 1)
                    nc.vector.scalar_tensor_tensor(h0_none, slot(0, 0), 1.0 / SCALE, none,
                                                   ALU.mult, ALU.mult).then_inc(s_none, 1)
                    dve.wait_ge(s_none, t * 3 + 2)
                    nc.vector.tensor_tensor(accT[:, col], accT[:, col], h0_none, ALU.add).then_inc(s_none, 1)
                    dve.wait_ge(s_none, t * 3 + 3)

                with dve.If(flag_dve == 0):
                    if l:
                        groups_and_chunks(dve, group, start_output, add_output, finish_output)
                        dve.wait_ge(s_acc[1], GROUPS + 1)
                    else:
                        dense_blocks()
                with dve.Else():
                    if l == 0:
                        dve.wait_ge(s_hlo, CHUNKS)
                        dve.wait_ge(s_tab[0], 2 * CHUNKS * 16)
                    pairs(dve, group_all_windows)
                    dve.wait_ge(s_acc[l], GROUPS * NW * (2 - l) + 1)
                    if l == 0:
                        with dve.Fori(0, TILES) as t:
                            no_edges(t)
                    else:
                        with dve.Fori(0, CHUNKS - 1) as c:
                            sums_to_products(1, c, 0)
                            add_output(c)
                            finish_output(c)

            def sums_to_products(l, c, j):
                nc.vector.tensor_copy(crcnt[:, j, :], rcnt[:, bass.ds(c * RING, RING)]).then_inc(s_rcnt[l], 1)
                nc.vector.tensor_copy(st_sums[j].rearrange("p j d -> p (j d)"),
                                      accT[:, bass.ds(c * (RING * P), RING * P)]).then_inc(s_st[l], 1)

            def add_products(l, c, j, bank):
                keep = (xs, hs)[l]
                dve.wait_ge(s_rcnt[l], c + 1)
                for t in range(RING):
                    dve.wait_ge(s_y[l], c * RING + bank_full(t))
                    nc.vector.scalar_tensor_tensor(keep[:, c * RING + t, :], slot(bank, t), crcnt[:, j, t:t + 1],
                                                   keep[:, c * RING + t, :], ALU.mult, ALU.add).then_inc(s_x1[l], 1)
                dve.wait_ge(s_x1[l], c * RING + RING)
                apart(dve)
                for t in range(RING):
                    nc.vector.bn_stats(cstats[:, t, :], keep[:, c * RING + t, :]).then_inc(s_bn[l], 1)
                dve.wait_ge(s_bn[l], c * RING + RING)
                steps = [0]

                def step(ins):
                    steps[0] += 1
                    ins.then_inc(s_step[l], 1)
                    dve.wait_ge(s_step[l], c * 4 + steps[0])

                spread(cstats, csmall, step).then_inc(s_var[l], 1)

            def scales(l, c):
                dve.wait_ge(s_std[l], c + 1)
                nc.vector.reciprocal(rstd1[:, :], csmall[:, 5, :]).then_inc(s_recip[l], 1)
                dve.wait_ge(s_recip[l], c + 1)
                nc.vector.scalar_tensor_tensor(nb1[:, :], csmall[:, 0, :], -0.5, rstd1[:, :],
                                               ALU.mult, ALU.mult).then_inc(s_nb[l], 1)

            def nodes(c, j, first, last):
                if first:
                    sums_to_products(0, 0, 0)
                if not last:
                    sums_to_products(0, c + 1, 1 - j)
                dve.wait_ge(s_xb, c + 1)
                add_products(0, c, j, 6 * j)
                if not first:
                    dve.wait_ge(s_h1, c * RING)
                    second_part(c - 1, c)
                scales(0, c)

            def second_part(c, count):
                dve.wait_ge(s_h1hi, count)
                nc.vector.scalar_tensor_tensor(h_lo[:, bass.ds(c * RING, RING), :], st_h, SCALE,
                                               h_hi[:, bass.ds(c * RING, RING), 0:D],
                                               ALU.mult, ALU.subtract).then_inc(s_h1lo, 1)

            def start_output(c):
                dve.wait_ge(s_acc[1], c * STRIDE + (STRIDE + 1))
                sums_to_products(1, c, 0)

            def add_output(c):
                add_products(1, c, 0, 4)

            def finish_output(c):
                scales(1, c)
                some = bass.ds(c * RING, RING)
                nc.vector.tensor_tensor(xs[:, some, :], xs[:, some, :], rows[:, 4:5, :].to_broadcast([P, RING, D]),
                                        ALU.add).then_inc(s_xl, 1)
                dve.wait_ge(s_z, c * RING + RING)
                nc.vector.tensor_tensor(st_t, st_h, rows[:, 3:4, :].to_broadcast([P, RING, D]),
                                        ALU.mult).then_inc(s_zg, 1)
                dve.wait_ge(s_xl, c + 1)
                dve.wait_ge(s_zg, c + 1)
                nc.vector.tensor_tensor(st_o, st_t, xs[:, some, :], ALU.add).then_inc(s_fin, 1)

            layer(0)
            counts = cntT[:, 0:TILES * P].rearrange("p (t q c) -> p t q c", q=4, c=32)
            for q in range(4):
                quarter = slice(32 * q, 32 * q + 32)
                nc.vector.transpose(turned[quarter], counts[quarter, :, q, :]).then_inc(s_turned, 1)
            dve.wait_ge(s_turned, 4)
            chain(nc.vector.tensor_scalar(rcnt[:, :], turned[:, :, 0], 1.0, None, ALU.max))
            chain(nc.vector.reciprocal(rcnt[:, :], rcnt[:, :]))
            chunks(dve, nodes)
            second_part(CHUNKS - 1, CHUNKS)
            dve.wait_ge(s_st[0], CHUNKS)
            nc.vector.memset(accT[:, :], 0.0).then_inc(s_acc[1], 1)
            dve.wait_ge(s_cps0, 1)
            chain(nc.vector.tensor_tensor(cmat[:, 0, :], slot(0, 0)[0:K3, :], msgbr[0:K3, :], ALU.add))
            chain(nc.vector.tensor_copy(cpart[:, 0, :], cmat[:, 0, :]))
            chain(nc.vector.tensor_tensor(cmat[:, 1, :], cmat[:, 0, :], cpart[:, 0, :], ALU.subtract))
            chain(nc.vector.tensor_copy(cpart[:, 1, :], cmat[:, 1, :]))
            chain(nc.vector.tensor_tensor(cmat[:, 2, :], cmat[:, 1, :], cpart[:, 1, :], ALU.subtract))
            chain(nc.vector.tensor_copy(cpart[:, 2, :], cmat[:, 2, :]))
            third = [kc[0:K3, KI + 1 + k:KI + 2 + k] for k in range(3)]
            chain(nc.vector.tensor_scalar(cmat[:, 0, :], cpart[:, 0, :], third[0], None, ALU.mult))
            chain(nc.vector.scalar_tensor_tensor(cmat[:, 1, :], cpart[:, 1, :], third[1], cmat[:, 0, :],
                                                 ALU.mult, ALU.add))
            nc.vector.scalar_tensor_tensor(csel[:, :], cpart[:, 2, :], third[2], cmat[:, 1, :],
                                           ALU.mult, ALU.add).then_inc(s_csel, 1)
            dve.wait_ge(s_keep, CHUNKS)
            chain(nc.vector.tensor_scalar(node_id, kc[:, P:P + RUN][:, :, None].to_broadcast([P, RUN, P]), float(P),
                                          kc[:, KI + 5:KI + 6], ALU.mult, ALU.add))
            pick_sources(0, 0, True)
            one_hot_types(0, 0)
            pick_sources(1, 1, False)
            layer(1)
            sums_to_products(1, CHUNKS - 1, 0)
            add_output(CHUNKS - 1)
            finish_output(CHUNKS - 1)


def kernel(x, src, dst, edge_type_16, L0_gnn_W, L0_gnn_b, L1_gnn_edge_emb_W, L1_gnn_msg_W, L1_gnn_msg_b,
           L1_gnn_upd_W, L1_gnn_upd_b, L1_gnn_ln_g, L1_gnn_ln_b):
    import numpy as np
    import concourse.bacc as bacc
    from concourse.bass_utils import run_bass_kernel_spmd

    x, src, dst, typ = (np.asarray(a) for a in (x, src, dst, edge_type_16))
    N, D = x.shape
    E = src.shape[0]
    per = TPG * P
    groups = -(-E // per)
    groups += groups % 2
    blocks = 8
    while (blocks // 2 + 2) * TPG0 + blocks * TPB < -(-E // P):
        blocks += 4
    groups0 = blocks // 2 + 2
    lead = groups0 * TPG0
    tiles = max(lead + (blocks + 1) * TPB, groups * TPG)

    def padded(a, value, n):
        return np.concatenate([a, np.full((n - E,), value, a.dtype)])

    def ends(start, size, count):
        first = np.minimum((start + np.arange(count) * size) * P, E - 1)
        return first, np.minimum(first + size * P, E) - 1

    src_p, typ_p = (padded(a, 0, groups * per) for a in (src, typ))
    src_q, dst_q = padded(src, 0, tiles * P), padded(dst, 1 << 20, tiles * P)
    gfirst, glast = ends(0, TPG, groups)
    gfirst0, glast0 = ends(0, TPG0, groups0)
    bfirst, blast = ends(lead, TPB, blocks + 1)
    tends = [np.append(dst[e], np.zeros(-tiles % P, dst.dtype)).reshape(-1, P).T for e in ends(0, 1, tiles)]
    tfirst = dst_q[::P]
    by_block = tfirst[lead:lead + (blocks + 1) * TPB].reshape(-1, TPB)
    niota = max(P, WB, -(-N // P) * WT + 3)
    consts = np.zeros((P, P + niota + 6), np.float32)
    consts[:, 0:P] = np.eye(P)
    consts[:, P:P + niota] = np.arange(niota)
    consts[:, P + niota] = np.arange(P) % 16
    for k in range(3):
        consts[16 * k:16 * k + 16, P + niota + 1 + k] = 1.0
    consts[:, P + niota + 4] = np.arange(P) % WT
    consts[:, P + niota + 5] = np.arange(P)
    pick = np.zeros((groups + 2, 1, P), src.dtype)
    pick[:groups] = src_p.reshape(groups, TPG, P)[:, TPG - 1:TPG]
    row = lambda a: np.asarray(a).reshape(1, -1)
    cols = lambda a: np.ascontiguousarray(np.asarray(a).T)
    msg_w = np.asarray(L1_gnn_msg_W)
    arrays = {
        "x": x,
        "idx_g": np.ascontiguousarray(src_p.reshape(groups, TPG, P).transpose(0, 2, 1)),
        "idx0_g": np.ascontiguousarray(src_q[:lead * P].reshape(groups0, TPG0, P).transpose(0, 2, 1)),
        "pick_g": pick,
        "src_t": np.ascontiguousarray(src_q.reshape(tiles, P).T),
        "dst_t": np.ascontiguousarray(dst_q.reshape(tiles, P).T),
        "dst_flat": dst,
        "tfirst": row(tfirst),
        "tfirst_p": np.ascontiguousarray(tends[0]),
        "tlast_p": np.ascontiguousarray(tends[1]),
        "bfirst": row(dst[bfirst]),
        "blast": row(dst[blast]),
        "trep": np.ascontiguousarray(np.repeat(by_block, WT, axis=1).T),
        "gfirst": row(dst[gfirst]),
        "glast": row(dst[glast]),
        "gfirst0": row(dst[gfirst0]),
        "glast0": row(dst[glast0]),
        "types_g": np.append(typ_p, np.zeros(per, typ.dtype)).reshape(groups + 1, 1, per),
        "w0t": cols(L0_gnn_W),
        "b0": row(L0_gnn_b),
        "embt": cols(L1_gnn_edge_emb_W),
        "wet": cols(msg_w[:, D:]),
        "wxt": cols(msg_w[:, :D]),
        "msgb": row(L1_gnn_msg_b),
        "updt": cols(L1_gnn_upd_W),
        "updb": row(L1_gnn_upd_b),
        "lng": row(L1_gnn_ln_g),
        "lnb": row(L1_gnn_ln_b),
        "consts": consts,
    }
    nc = bacc.Bacc("TRN2", target_bir_lowering=False, num_devices=1)
    args = [nc.dram_tensor(k, a.shape, mybir.dt.from_np(a.dtype), kind="ExternalInput").ap()
            for k, a in arrays.items()]
    out = nc.dram_tensor("out", (N, D), F32, kind="ExternalOutput").ap()
    gnn_program(nc, *args, out, E)
    r = run_bass_kernel_spmd(nc, [arrays], core_ids=[0])
    return r.results[0]["out"]
```
